# Optimizing a Trainium2 kernel written in Bass

```python
import numpy as np
import jax
import jax.numpy as jnp

def _softmax(x, axis=-1):
    return jax.nn.softmax(x, axis=axis)

def _gelu(x):
    return jax.nn.gelu(x, approximate=True)

def _silu(x):
    return jax.nn.silu(x)

def _sigmoid(x):
    return jax.nn.sigmoid(x)

def _layernorm(x, axis=-1, eps=1e-05):
    m = jnp.mean(x, axis=axis, keepdims=True)
    v = jnp.var(x, axis=axis, keepdims=True)
    return (x - m) / jnp.sqrt(v + eps)

def _scatter_add(tgt, idx, src, axis=0):
    return tgt.at[idx].add(src)

def _segment_sum(src, seg, n):
    return jax.ops.segment_sum(src, seg, n)
kernel_name = 'mk_gnn_preln_d4_gnn_r8_dcecb0'

def setup_inputs(seed: int=0):
    np.random.seed(seed)
    _w = jnp.asarray

    def _rec_inputs():
        import jax
        import jax.numpy as jnp
        _gk = jax.random.key(seed)
        x = -0.0003713 + 1 * jax.random.normal(jax.random.fold_in(_gk, 1), (6250, 128), jnp.float32)
        _s = jax.random.randint(jax.random.fold_in(_gk, 2), (50000,), 0, 6250, jnp.int32)
        _d = jax.random.randint(jax.random.fold_in(_gk, 3), (50000,), 0, 6250, jnp.int32)
        _loop = jnp.arange(6250, dtype=jnp.int32)
        src = jnp.concatenate([_s, _d, _loop])
        dst = jnp.concatenate([_d, _s, _loop])
        _o = jnp.argsort(dst, stable=True)
        src = src[_o]
        dst = dst[_o]
        edge_attr_20 = jax.random.uniform(jax.random.fold_in(_gk, 12), (106250, 20), jnp.float32, 0.0, 1)
        edge_weight = jax.random.uniform(jax.random.fold_in(_gk, 14), (106250,), jnp.float32, 0.0, 0.999998)
        return (x, src, dst, edge_attr_20, edge_weight)
    x, src, dst, edge_attr_20, edge_weight = _rec_inputs()

    def _L0_gnn_setup():
        import jax, jax.numpy as jnp
        import numpy as np
        N_NODES = 12500
        N_EDGES = 200000
        D_IN = 128
        D_OUT = 128
        BN_EPS = 1e-05
        key = jax.random.key(seed)
        ks = jax.random.split(key, 6)
        X = jax.random.normal(ks[0], (N_NODES, D_IN), dtype=jnp.float32)
        W = jax.random.normal(ks[1], (D_OUT, D_IN), dtype=jnp.float32) * (1.0 / np.sqrt(D_IN))
        b = jax.random.normal(ks[2], (D_OUT,), dtype=jnp.float32) * 0.01
        gamma = jnp.ones((D_OUT,), dtype=jnp.float32)
        beta = jnp.zeros((D_OUT,), dtype=jnp.float32)
        src = jax.random.randint(ks[3], (N_EDGES,), 0, N_NODES, dtype=jnp.int64 if jax.config.read('jax_enable_x64') else jnp.int32)
        dst = jax.random.randint(ks[4], (N_EDGES,), 0, N_NODES, dtype=jnp.int64 if jax.config.read('jax_enable_x64') else jnp.int32)
        return {'X': X, 'W': W, 'b': b, 'gamma': gamma, 'beta': beta, 'src': src, 'dst': dst}
    _L0_gnn_all = _L0_gnn_setup()
    _L0_gnn_in = {k: v for k, v in _L0_gnn_all.items() if k in ('W', 'b', 'gamma', 'beta')}
    del _L0_gnn_all

    def _L1_gnn_setup():
        import jax, jax.numpy as jnp
        import numpy as np
        from jax.scipy.special import erf
        N_NODES = 6250
        N_EDGES = 100000
        N_BASIS = 128
        N_RBF = 20
        N_FILT = 128

        def smu(x, alpha=0.01, mu=2.5):
            return ((1 + alpha) * x + (1 - alpha) * x * erf(mu * (1 - alpha) * x)) / 2
        key = jax.random.key(seed)
        ks = jax.random.split(key, 16)
        x = jax.random.normal(ks[0], (N_NODES, N_BASIS), dtype=jnp.float32)
        f_ij = jax.random.uniform(ks[1], (N_EDGES, N_RBF), dtype=jnp.float32)
        rcut_ij = jax.random.uniform(ks[2], (N_EDGES,), dtype=jnp.float32)
        idx_i = jnp.sort(jax.random.randint(ks[3], (N_EDGES,), 0, N_NODES))
        idx_j = jax.random.randint(ks[4], (N_EDGES,), 0, N_NODES)
        s = lambda n: 1.0 / np.sqrt(n)
        W_in2f = jax.random.normal(ks[5], (N_FILT, N_BASIS), dtype=jnp.float32) * s(N_BASIS)
        W_f1 = jax.random.normal(ks[6], (N_FILT, N_RBF), dtype=jnp.float32) * s(N_RBF)
        b_f1 = jnp.zeros((N_FILT,), jnp.float32)
        W_f2 = jax.random.normal(ks[7], (N_FILT, N_FILT), dtype=jnp.float32) * s(N_FILT)
        b_f2 = jnp.zeros((N_FILT,), jnp.float32)
        W_o1 = jax.random.normal(ks[8], (N_BASIS, N_FILT), dtype=jnp.float32) * s(N_FILT)
        b_o1 = jnp.zeros((N_BASIS,), jnp.float32)
        W_o2 = jax.random.normal(ks[9], (N_BASIS, N_BASIS), dtype=jnp.float32) * s(N_BASIS)
        b_o2 = jnp.zeros((N_BASIS,), jnp.float32)
        return dict(x=x, f_ij=f_ij, rcut_ij=rcut_ij, idx_i=idx_i, idx_j=idx_j, W_in2f=W_in2f, W_f1=W_f1, b_f1=b_f1, W_f2=W_f2, b_f2=b_f2, W_o1=W_o1, b_o1=b_o1, W_o2=W_o2, b_o2=b_o2)
    _L1_gnn_all = _L1_gnn_setup()
    _L1_gnn_in = {k: v for k, v in _L1_gnn_all.items() if k in ('W_in2f', 'W_f1', 'b_f1', 'W_f2', 'b_f2', 'W_o1', 'b_o1', 'W_o2', 'b_o2')}
    del _L1_gnn_all

    def _L2_gnn_setup():
        import jax, jax.numpy as jnp
        import numpy as np
        N_NODES = 6250
        N_EDGES = 75000
        FEAT = 128
        N_LAYERS = 4

        def _edgeconv(x, src, dst, tw, tb, pw, pb):
            phi = x @ pw.T + pb
            diff = x[src] - x[dst]
            msg = diff @ tw.T + tb + phi[dst]
            agg = jax.ops.segment_max(msg, dst, num_segments=x.shape[0])
            return jnp.where(jnp.isneginf(agg), jnp.zeros_like(agg), agg)
        key = jax.random.key(seed)
        ks = jax.random.split(key, 7)
        feats = jax.random.normal(ks[0], (N_NODES, FEAT), dtype=jnp.float32)
        src = jax.random.randint(ks[1], (N_EDGES,), 0, N_NODES)
        dst = jax.random.randint(ks[2], (N_EDGES,), 0, N_NODES)
        s = 1.0 / np.sqrt(FEAT)
        theta_w = jax.random.uniform(ks[3], (N_LAYERS, FEAT, FEAT), jnp.float32, -s, s)
        theta_b = jax.random.uniform(ks[4], (N_LAYERS, FEAT), jnp.float32, -s, s)
        phi_w = jax.random.uniform(ks[5], (N_LAYERS, FEAT, FEAT), jnp.float32, -s, s)
        phi_b = jax.random.uniform(ks[6], (N_LAYERS, FEAT), jnp.float32, -s, s)
        return {'feats': feats, 'src': src, 'dst': dst, 'theta_w': theta_w, 'theta_b': theta_b, 'phi_w': phi_w, 'phi_b': phi_b}
    _L2_gnn_all = _L2_gnn_setup()
    _L2_gnn_in = {k: v for k, v in _L2_gnn_all.items() if k in ('theta_w', 'theta_b', 'phi_w', 'phi_b')}
    del _L2_gnn_all

    def _L3_gnn_setup():
        import jax, jax.numpy as jnp
        import numpy as np
        N_NODES = 12500
        N_EDGES = 200000
        D_IN = 128
        D_HID = 128

        def gcn_conv(x, src, dst, W, b, n_nodes):
            deg = jax.ops.segment_sum(jnp.ones_like(src, dtype=x.dtype), dst, num_segments=n_nodes)
            dinv = jnp.where(deg > 0, deg ** (-0.5), 0.0)
            norm = dinv[src] * dinv[dst]
            h = x @ W
            msg = h[src] * norm[:, None]
            out = jax.ops.segment_sum(msg, dst, num_segments=n_nodes)
            return out + b
        key = jax.random.key(seed)
        k1, k2, k3, k4 = jax.random.split(key, 4)
        x = jax.random.normal(k1, (N_NODES, D_IN), dtype=jnp.float32)
        edge_index = jax.random.randint(k2, (2, N_EDGES), 0, N_NODES, dtype=jnp.int64)
        s1 = (1.0 / np.sqrt(D_IN)).astype(np.float32)
        s2 = (1.0 / np.sqrt(D_HID)).astype(np.float32)
        W1 = jax.random.normal(k3, (D_IN, D_HID), dtype=jnp.float32) * s1
        b1 = jnp.zeros((D_HID,), dtype=jnp.float32)
        W2 = jax.random.normal(k4, (D_HID, D_HID), dtype=jnp.float32) * s2
        b2 = jnp.zeros((D_HID,), dtype=jnp.float32)
        return {'x': x, 'edge_index': edge_index, 'W1': W1, 'b1': b1, 'W2': W2, 'b2': b2}
    _L3_gnn_all = _L3_gnn_setup()
    _L3_gnn_in = {k: v for k, v in _L3_gnn_all.items() if k in ('W1', 'b1', 'W2', 'b2')}
    del _L3_gnn_all
    return {'x': x, 'src': src, 'dst': dst, 'edge_attr_20': edge_attr_20, 'edge_weight': edge_weight, 'L0_gnn_W': _L0_gnn_in['W'], 'L0_gnn_b': _L0_gnn_in['b'], 'L0_gnn_gamma': _L0_gnn_in['gamma'], 'L0_gnn_beta': _L0_gnn_in['beta'], 'L1_gnn_W_in2f': _L1_gnn_in['W_in2f'], 'L1_gnn_W_f1': _L1_gnn_in['W_f1'], 'L1_gnn_b_f1': _L1_gnn_in['b_f1'], 'L1_gnn_W_f2': _L1_gnn_in['W_f2'], 'L1_gnn_b_f2': _L1_gnn_in['b_f2'], 'L1_gnn_W_o1': _L1_gnn_in['W_o1'], 'L1_gnn_b_o1': _L1_gnn_in['b_o1'], 'L1_gnn_W_o2': _L1_gnn_in['W_o2'], 'L1_gnn_b_o2': _L1_gnn_in['b_o2'], 'L2_gnn_theta_w': _L2_gnn_in['theta_w'], 'L2_gnn_theta_b': _L2_gnn_in['theta_b'], 'L2_gnn_phi_w': _L2_gnn_in['phi_w'], 'L2_gnn_phi_b': _L2_gnn_in['phi_b'], 'L3_gnn_W1': _L3_gnn_in['W1'], 'L3_gnn_b1': _L3_gnn_in['b1'], 'L3_gnn_W2': _L3_gnn_in['W2'], 'L3_gnn_b2': _L3_gnn_in['b2']}

def reference(x, src, dst, edge_attr_20, edge_weight, L0_gnn_W, L0_gnn_b, L0_gnn_gamma, L0_gnn_beta, L1_gnn_W_in2f, L1_gnn_W_f1, L1_gnn_b_f1, L1_gnn_W_f2, L1_gnn_b_f2, L1_gnn_W_o1, L1_gnn_b_o1, L1_gnn_W_o2, L1_gnn_b_o2, L2_gnn_theta_w, L2_gnn_theta_b, L2_gnn_phi_w, L2_gnn_phi_b, L3_gnn_W1, L3_gnn_b1, L3_gnn_W2, L3_gnn_b2):
    import jax
    import jax.numpy as jnp

    def _L0_gnn_ref(X, W, b, gamma, beta, src, dst):
        import jax, jax.numpy as jnp
        import numpy as np
        N_NODES = 12500
        N_EDGES = 200000
        D_IN = 128
        D_OUT = 128
        BN_EPS = 1e-05
        H = X @ W.T + b
        mu = jnp.mean(H, axis=0)
        var = jnp.mean(jnp.square(H - mu), axis=0)
        H = (H - mu) * jax.lax.rsqrt(var + BN_EPS) * gamma + beta
        n = X.shape[0]
        ones = jnp.ones(dst.shape, dtype=H.dtype)
        deg_hat = 1.0 + jax.ops.segment_sum(ones, dst, num_segments=n)
        dinv = jax.lax.rsqrt(deg_hat)
        norm = dinv[src] * dinv[dst]
        msg = H[src] * norm[:, None]
        out = jax.ops.segment_sum(msg, dst, num_segments=n)
        out = out + H * (dinv * dinv)[:, None]
        return jax.nn.relu(out)

    def _L1_gnn_ref(x, f_ij, rcut_ij, idx_i, idx_j, W_in2f, W_f1, b_f1, W_f2, b_f2, W_o1, b_o1, W_o2, b_o2):
        import jax, jax.numpy as jnp
        import numpy as np
        from jax.scipy.special import erf
        N_NODES = 6250
        N_EDGES = 100000
        N_BASIS = 128
        N_RBF = 20
        N_FILT = 128

        def smu(x, alpha=0.01, mu=2.5):
            return ((1 + alpha) * x + (1 - alpha) * x * erf(mu * (1 - alpha) * x)) / 2
        h = x @ W_in2f.T
        Wij = smu(f_ij @ W_f1.T + b_f1) @ W_f2.T + b_f2
        Wij = Wij * rcut_ij[:, None]
        x_ij = h[idx_j] * Wij
        agg = jax.ops.segment_sum(x_ij, idx_i, num_segments=h.shape[0])
        out = smu(agg @ W_o1.T + b_o1) @ W_o2.T + b_o2
        return out

    def _L2_gnn_ref(feats, src, dst, theta_w, theta_b, phi_w, phi_b):
        import jax, jax.numpy as jnp
        import numpy as np
        N_NODES = 6250
        N_EDGES = 75000
        FEAT = 128
        N_LAYERS = 4

        def _edgeconv(x, src, dst, tw, tb, pw, pb):
            phi = x @ pw.T + pb
            diff = x[src] - x[dst]
            msg = diff @ tw.T + tb + phi[dst]
            agg = jax.ops.segment_max(msg, dst, num_segments=x.shape[0])
            return jnp.where(jnp.isneginf(agg), jnp.zeros_like(agg), agg)
        x = feats
        for l in range(N_LAYERS):
            x = _edgeconv(x, src, dst, theta_w[l], theta_b[l], phi_w[l], phi_b[l])
            x = jax.nn.relu(x)
        return x

    def _L3_gnn_ref(x, edge_index, W1, b1, W2, b2):
        import jax, jax.numpy as jnp
        import numpy as np
        N_NODES = 12500
        N_EDGES = 200000
        D_IN = 128
        D_HID = 128

        def gcn_conv(x, src, dst, W, b, n_nodes):
            deg = jax.ops.segment_sum(jnp.ones_like(src, dtype=x.dtype), dst, num_segments=n_nodes)
            dinv = jnp.where(deg > 0, deg ** (-0.5), 0.0)
            norm = dinv[src] * dinv[dst]
            h = x @ W
            msg = h[src] * norm[:, None]
            out = jax.ops.segment_sum(msg, dst, num_segments=n_nodes)
            return out + b
        n_nodes = x.shape[0]
        loops = jnp.arange(n_nodes, dtype=edge_index.dtype)
        src = jnp.concatenate([edge_index[0], loops])
        dst = jnp.concatenate([edge_index[1], loops])
        h = gcn_conv(x, src, dst, W1, b1, n_nodes)
        h = gcn_conv(h, src, dst, W2, b2, n_nodes)
        return h
    edge_index = jnp.stack([src, dst])
    h = jnp.maximum(_layernorm(x, axis=-1), 0.0)
    x = x + _L0_gnn_ref(h, L0_gnn_W, L0_gnn_b, L0_gnn_gamma, L0_gnn_beta, src, dst)
    h = jnp.maximum(_layernorm(x, axis=-1), 0.0)
    x = x + _L1_gnn_ref(h, edge_attr_20, edge_weight, src, dst, L1_gnn_W_in2f, L1_gnn_W_f1, L1_gnn_b_f1, L1_gnn_W_f2, L1_gnn_b_f2, L1_gnn_W_o1, L1_gnn_b_o1, L1_gnn_W_o2, L1_gnn_b_o2)
    h = jnp.maximum(_layernorm(x, axis=-1), 0.0)
    x = x + _L2_gnn_ref(h, src, dst, L2_gnn_theta_w, L2_gnn_theta_b, L2_gnn_phi_w, L2_gnn_phi_b)
    h = jnp.maximum(_layernorm(x, axis=-1), 0.0)
    x = x + _L3_gnn_ref(h, edge_index, L3_gnn_W1, L3_gnn_b1, L3_gnn_W2, L3_gnn_b2)
    return x

_drawn_inputs = setup_inputs


def setup_inputs(seed=0):
    import zlib

    import numpy as np

    out = dict(_drawn_inputs(seed))
    spreads = {'L0_gnn_gamma': (1.0, 0.2),
     'L0_gnn_beta': (0.0, 0.1),
     'L1_gnn_b_f1': (0.0, 0.1),
     'L1_gnn_b_f2': (0.0, 0.1),
     'L1_gnn_b_o1': (0.0, 0.1),
     'L1_gnn_b_o2': (0.0, 0.1),
     'L3_gnn_b1': (0.0, 0.1),
     'L3_gnn_b2': (0.0, 0.1)}
    factors = {}
    for name, (base, spread) in spreads.items():
        noise = np.random.default_rng([zlib.crc32(name.encode()), seed]).standard_normal(out[name].shape)
        drawn = base * np.exp(spread * noise) if base else spread * noise
        out[name] = jnp.asarray(drawn.astype(out[name].dtype))
    for name, factor in factors.items():
        out[name] = (out[name] * factor).astype(out[name].dtype)
    return out
```

```python
import concourse.bass as bass
from concourse import mybir
from contextlib import ExitStack

P = 128
N = 6250
E = 106250
F = 128
K_ATTR = 20
NT = -(-N // P)
N_PAD = NT * P
GROUP = 7
NG = NT // GROUP
GN = GROUP * P
UNROLL = 32
HALF = 16
T = -(-E // (P * UNROLL)) * UNROLL
ITERS = T // UNROLL
E_PAD = P * T
FULL = E // T
REST = E - FULL * T
RING = 8
QUAD = 4
QUADS = T // QUAD
CQ = HALF // QUAD
ACCS = 4
TB = -(-T // P)
BIG = 1.0e38
EPS = 1e-5
ALPHA = 0.01
SMU_S = 2.0 ** 0.5 * 2.5 * (1 - ALPHA)
SMU_G = (1 - ALPHA) / SMU_S
ROW_SUM = E_PAD
ROW_MAX = E_PAD + 1
LAYERS = 4
KA = QUAD * K_ATTR + 1
NW = 5 + 2 * LAYERS


def gnn_kernel(nc, x, src, dst, edge_attr, edge_weight, w0, b0, gamma, beta, w_in2f, w_f1, b_f1,
               w_f2, b_f2, w_o1, b_o1, w_o2, b_o2, theta_w, theta_b, phi_w, phi_b, w1, b1, w2, b2, out):
    f32, i32, u32, bf16 = mybir.dt.float32, mybir.dt.int32, mybir.dt.uint32, mybir.dt.bfloat16
    ALU = mybir.AluOpType
    ACT = mybir.ActivationFunctionType
    ds = bass.ds
    ctx = ExitStack()
    with ctx:
        def sb(name, shape, dt=f32):
            return ctx.enter_context(nc.sbuf_tensor(name, shape, dt))

        def dram(name, shape, dt=f32):
            return nc.dram_tensor(name, shape, dt, kind="Internal").ap()

        cleared = []

        def sem(name, phase=True):
            s = ctx.enter_context(nc.semaphore(name))
            if phase:
                cleared.append(s)
            return s

        def wait(eng, s, value):
            if not isinstance(value, int) or value > 0:
                eng.wait_ge(s, value)

        def hold(eng, s, value):
            if not isinstance(value, int) or value > 0:
                eng.wait_ge(s, value)
                if not isinstance(value, int):
                    eng.sem_inc(held[eng.engine], 1)

        table = dram("table", (N_PAD, F))
        run_rows = dram("run_rows", (E_PAD + 2, F))
        fill_rows = dram("fill_rows", (E_PAD + P, F))
        attr_pad = dram("attr_pad", (E_PAD, K_ATTR))
        src_rows = dram("src_rows", (2, T * P), bf16)
        acc_dram = [dram(f"acc{k}", (N_PAD + P, F)) for k in range(ACCS)]
        run_view = run_rows[0:E_PAD, :].rearrange("(p t) f -> p (t f)", t=T)
        fill_view = fill_rows[0:E_PAD, :].rearrange("(p t) f -> p (t f)", t=T)

        X = sb("X", [P, NT, F])
        TBL = sb("TBL", [P, NT, F])
        BASE = sb("BASE", [P, NT, F])
        HT = BASE[:, :, :].rearrange("p a b -> p (a b)")
        KEEP = sb("KEEP", [P, T])
        RESET = sb("RESET", [P, T])
        WEIGHT = sb("WEIGHT", [P, T])
        SRCF = sb("SRCF", [P, T])
        SCAT = sb("SCAT", [P, T])
        ident = sb("ident", [P, P])
        ones = sb("ones", [P, P])
        ones_bf = sb("ones_bf", [2, P], bf16)
        lower = sb("lower", [P, P])
        iota_p = sb("iota_p", [P, 1])
        iota_bf = sb("iota_bf", [P, P], bf16)
        iota_i = sb("iota_i", [P, P], i32)
        iota_pi = sb("iota_pi", [P, 1], i32)
        zeros = sb("zeros", [P, HALF * F])
        neutral = sb("neutral", [2, F])
        WORK = sb("WORK", [P, 4 * HALF * F])
        RUN = WORK[:, 0:2 * HALF * F].rearrange("p (h t f) -> p h t f", h=2, t=HALF)
        FILL = WORK[:, 2 * HALF * F:].rearrange("p (h t f) -> p h t f", h=2, t=HALF)
        ACC = WORK[:, 0:2 * ACCS * GROUP * F].rearrange("p (s k t f) -> p s k t f", s=2, k=ACCS, t=GROUP)

        def field(k, dt=f32):
            v = WORK[:, k * (T + 8):k * (T + 8) + T + 1]
            return v if dt == f32 else v.bitcast(dt)

        SRC, DP, LOI, HII = (field(k, i32) for k in range(4))
        SRC_LO, SRC_HI, DSTF = (field(k) for k in range(4, 7))
        LOB, HIB = field(7, bf16), field(8, bf16)
        deg = sb("deg", [P, NT])
        dinv = sb("dinv", [P, NT])
        tmpn = sb("tmpn", [P, 8, NT])
        idx_sum = sb("idx_sum", [P, NT], i32)
        idx_max = sb("idx_max", [P, NT], i32)
        idx_first = sb("idx_first", [P, NT], i32)
        seg = sb("seg", [P, 4])
        idx_patch = sb("idx_patch", [P, 1], i32)
        first_dst = sb("first_dst", [P, 1], i32)
        cont_cols = sb("cont_cols", [P, 2, P])
        CONT = sb("CONT", [P, P])
        CHAIN = sb("CHAIN", [P, P])
        CONT_R = sb("CONT_R", [P, P])
        CHAIN_R = sb("CHAIN_R", [P, P])
        upper = CONT_R
        stage = sb("stage", [P, 2, HALF], i32)
        G = sb("G", [P, RING, F])
        carry_t = sb("carry_t", [P, 2, P])
        patch = sb("patch", [P, 2, F])
        NR = sb("NR", [P, 2, GROUP, F])
        FE = sb("FE", [P, 2, GROUP, F])
        FT = sb("FT", [P, 2, GN])
        raw = NR[:, :, :, :].rearrange("p a b f -> p (a b) f")
        stats = sb("stats", [P, 2 * NG, 6])
        mv = sb("mv", [P, 2, GROUP, 2])
        norm = sb("norm", [P, 2, 3, GROUP])
        bnp = sb("bnp", [P, 8])
        WT = sb("WT", [P, 2, F])
        WO1 = sb("WO1", [P, F])
        WO2G = sb("WO2G", [P, F])
        WO2L = sb("WO2L", [P, F])
        WF2G = sb("WF2G", [P, F])
        WF2L = sb("WF2L", [P, F])
        WE = sb("WE", [P, LAYERS, 2 * F])
        W12 = sb("W12", [P, 2, F])
        cols = sb("cols", [P, 6])
        rowb = sb("rowb", [1, 4 + 2 * LAYERS, F])
        bias_o2 = sb("bias_o2", [P, F])
        bias_g = sb("bias_g", [P, 2, F])
        bias_e = sb("bias_e", [P, LAYERS, F])
        WB = sb("WB", [P, QUAD, KA])
        wf1 = sb("wf1", [P, K_ATTR])
        W1Q = sb("W1Q", [KA, QUAD, F])
        W21Q = sb("W21Q", [KA, QUAD, F])
        pick_one = sb("pick_one", [1, KA])
        AT = sb("AT", [P, 2, CQ, KA])
        ATT = sb("ATT", [KA, 4, P])
        GH = FT[:, :, 0:QUAD * P]
        HX = BASE[:, 0:2 * QUAD, :]
        MSG = BASE[:, 2 * QUAD:4 * QUAD, :].rearrange("p (s j) f -> p s j f", s=2)
        SAME = BASE[:, 4 * QUAD:8 * QUAD, :].rearrange("p (s j) f -> p s j f", s=4)
        TOT = sb("TOT", [P, 2, QUAD * F])
        SROW = sb("SROW", [2, 2, HALF * P], bf16)

        banks = [ctx.enter_context(nc.psum_tensor(f"bank{i}", [P, 1024], f32)) for i in range(4)]

        def bank(i, n=1):
            return banks[i // 2][:, i % 2 * 512:(i % 2 + n) * 512]

        loads_s, loads_a, consts = sem("loads_s"), sem("loads_a"), sem("consts")
        order_v, order_p, order_a = sem("order_v"), sem("order_p"), sem("order_a")
        pe_done, cp_done = sem("pe_done"), sem("cp_done")
        hot, counted = sem("hot"), sem("counted")
        staged, reduced = sem("staged"), sem("reduced")
        stored = [sem(f"stored{i}") for i in range(2)]
        zeroed = [sem(f"zeroed{i}") for i in range(2)]
        rows_in = [sem(f"rows_in{i}") for i in range(2)]
        fill_in = [sem(f"fill_in{i}") for i in range(2)]
        attr_in = [sem(f"attr_in{i}") for i in range(2)]
        acc_in = [sem(f"acc_in{i}") for i in range(2)]
        spread, compared = sem("spread"), sem("compared")
        attr_turned, attr_sb = sem("attr_turned"), sem("attr_sb")
        hidden, gelu_done, filtered = sem("hidden"), sem("gelu_done"), sem("filtered")
        expanded, messaged = sem("expanded"), sem("messaged")
        summed, totalled = sem("summed"), sem("totalled")
        held = {e.engine: sem(f"held_{n}") for n, e in (("sp", nc.sync), ("pool", nc.gpsimd))}
        rows_used, var_ready, std_ready = sem("rows_used"), sem("var_ready"), sem("std_ready")
        norm_ready, feat_ready = sem("norm_ready"), sem("feat_ready")
        turned, turned_sb = sem("turned"), sem("turned_sb")
        projected, table_ready, evicted = sem("projected"), sem("table_ready"), sem("evicted")
        table_out = sem("table_out")
        landed = [sem(f"landed{i}", phase=False) for i in range(RING)]
        rows_landed = [sem(f"rows_landed{i}", phase=False) for i in range(2)]
        patched = sem("patched", phase=False)
        firsts = sem("firsts", phase=False)
        added = [sem(f"added{k}", phase=False) for k in range(ACCS)]

        class Total:
            gathers = 0
            rows = [0, 0]
            patches = 0

        total = Total()

        def clear():
            with nc.Block() as block:
                @block.sync
                def _(sp):
                    for s in cleared:
                        sp.sem_clear(s)

        class Steps:
            def __init__(self, eng, s):
                self.eng, self.s, self.n = eng, s, 0

            def did(self, ins):
                self.n += 1
                return ins.then_inc(self.s, 1)

            def join(self):
                wait(self.eng, self.s, self.n)

            def then(self, ins):
                self.did(ins)
                self.join()

        with nc.Block() as block:
            @block.gpsimd
            def _(pool):
                pool.memset(SRC[:, 0:T], 0).then_inc(consts, 1)
                pool.memset(DP[:, 1:T + 1], N).then_inc(consts, 1)
                pool.memset(DP[:, 0:1], -1).then_inc(consts, 1)
                pool.memset(WEIGHT[:], 0.0).then_inc(consts, 1)
                st = Steps(pool, order_p)
                st.did(pool.memset(ones[:], 1.0))
                st.did(pool.iota(iota_pi[:], [[1, 1]], base=0, channel_multiplier=1))
                st.did(pool.iota(iota_i[:], [[1, P]], base=0, channel_multiplier=0))
                st.join()
                pool.affine_select(out=ident[:], in_=ones[:], compare_op=ALU.is_equal, fill=0.0,
                                   base=0, pattern=[[-1, P]], channel_multiplier=1)
                pool.affine_select(out=lower[:], in_=ones[:], compare_op=ALU.is_ge, fill=0.0,
                                   base=0, pattern=[[-1, P]], channel_multiplier=1)
                pool.affine_select(out=upper[:], in_=ones[:], compare_op=ALU.is_ge, fill=0.0,
                                   base=0, pattern=[[1, P]], channel_multiplier=-1)

            @block.vector
            def _(dve):
                dve.memset(X[:, NT - 1, :], 0.0).then_inc(consts, 1)
                dve.memset(zeros[:], 0.0)
                dve.memset(neutral[:], -BIG)
                dve.memset(ones_bf[:], 1.0)
                dve.memset(pick_one[:], 0.0)
                dve.memset(WB[:], 0.0)
                dve.memset(AT[:], 1.0)

            @block.sync
            def _(sp):
                n = 0

                def load(o, i, single=False):
                    nonlocal n
                    sp.dma_start(o, i, allow_slow_non_contiguous=single).then_inc(loads_s, 16)
                    n += 16

                sp.wait_ge(consts, 5)
                cut = FULL // 16 * 16
                for o, i in [(DP[:, 1:T + 1], dst), (SRC[:, 0:T], src), (WEIGHT[:, :], edge_weight)]:
                    load(o[0:cut, :], i[0:cut * T].rearrange("(p t) -> p t", t=T))
                    load(o[cut:FULL, :], i[cut * T:FULL * T].rearrange("(p t) -> p t", t=T))
                    load(o[FULL:FULL + 1, 0:REST], i[FULL * T:E].rearrange("(p t) -> p t", p=1))
                load(DP[1:FULL + 1, 0:1], dst[0:FULL * T].rearrange("(p t) -> p t", t=T)[:, T - 1:T], True)
                load(X[:, 0:NT - 1, :], x[0:(NT - 1) * P, :].rearrange("(t p) f -> p t f", p=P))
                load(X[0:N - (NT - 1) * P, NT - 1, :], x[(NT - 1) * P:N, :])
                sp.wait_ge(loads_s, n)

            @block.scalar
            def _(act):
                n = 0

                def load(o, i, single=False):
                    nonlocal n
                    act.dma_start(o, i, allow_slow_non_contiguous=single).then_inc(loads_a, 16)
                    n += 16

                for k, w in enumerate([w0, w_in2f, w_f2, w_o1, w_o2]):
                    load(raw[:, k, :], w)
                load(raw[:, 5:5 + LAYERS, :], theta_w.rearrange("l o i -> o l i"))
                load(raw[:, 5 + LAYERS:NW, :], phi_w.rearrange("l o i -> o l i"))
                load(wf1[:], w_f1)
                load(W12[:, 0, :], w1)
                load(W12[:, 1, :], w2)
                for k, b in enumerate([b0, gamma, beta, b_f1, b_o1]):
                    load(cols[:, k:k + 1], b.rearrange("(p a) -> p a", a=1))
                for k, b in enumerate([b_f2, b_o2, b1, b2]):
                    load(rowb[:, k, :], b.rearrange("(a n) -> a n", a=1))
                load(rowb[:, 4:4 + LAYERS, :], theta_b.rearrange("(a l) n -> a l n", a=1))
                load(rowb[:, 4 + LAYERS:, :], phi_b.rearrange("(a l) n -> a l n", a=1))
                act.wait_ge(loads_a, n)
        clear()

        with nc.Block() as block:
            @block.tensor
            def _(pe):
                for k in range(NW):
                    wait(pe, cp_done, k - 3)
                    nc.tensor.transpose(bank(k % 4)[:, 0:F], raw[:, k, :], ident[:]).then_inc(pe_done, 1)
                for k in range(3):
                    nc.tensor.matmul(bank(4)[:, k * F:(k + 1) * F], ones[0:1, :], rowb[:, 1 + k, :],
                                     start=True, stop=True)
                for l in range(LAYERS):
                    for k, first in ((4 + l, True), (4 + LAYERS + l, False)):
                        m = nc.tensor.matmul(bank(5)[:, l * F:(l + 1) * F], ones[0:1, :], rowb[:, k, :],
                                             start=first, stop=not first)
                m.then_inc(pe_done, 1)
                pe.wait_ge(order_p, 1)
                pe.wait_ge(cp_done, NW)
                for j in range(QUAD):
                    nc.tensor.transpose(bank(j)[0:KA, 0:F], WB[:, j, :], ident[:])
                    nc.tensor.matmul(bank(4 + j)[0:KA, 0:F] if j > 1 else bank(j)[0:KA, F:2 * F],
                                     WB[:, j, :], WF2L[:], start=True, stop=False)
                    m = nc.tensor.matmul(bank(4 + j)[0:KA, 0:F] if j > 1 else bank(j)[0:KA, F:2 * F],
                                         pick_one[:], rowb[:, 0, :], start=False, stop=True)
                m.then_inc(pe_done, 1)

            @block.scalar
            def _(act):
                for k in range(NW):
                    act.wait_ge(pe_done, k + 1)
                    p = bank(k % 4)[:, 0:F]
                    if k < 2:
                        last = act.copy(WT[:, k, :], p)
                    elif k in (2, 4):
                        g, lin = (WF2G, WF2L) if k == 2 else (WO2G, WO2L)
                        act.activation(g[:], p, ACT.Copy, scale=SMU_G)
                        last = act.activation(lin[:], p, ACT.Copy, scale=ALPHA)
                    elif k == 3:
                        last = act.copy(WO1[:], p)
                    else:
                        which, l = divmod(k - 5, LAYERS)
                        last = act.copy(WE[:, l, which * F:(which + 1) * F], p)
                    last.then_inc(cp_done, 1)
                act.wait_ge(pe_done, NW + 1)
                act.copy(bias_o2[:], bank(4)[:, 0:F])
                act.copy(bias_g[:, :, :].rearrange("p a b -> p (a b)"), bank(4)[:, F:3 * F])
                act.copy(bias_e[:, :, :].rearrange("p a b -> p (a b)"), bank(5))
                act.wait_ge(pe_done, NW + 2)
                for j in range(QUAD):
                    act.copy(W1Q[:, j, :], bank(j)[0:KA, 0:F])
                    act.copy(W21Q[:, j, :], bank(4 + j)[0:KA, 0:F] if j > 1 else bank(j)[0:KA, F:2 * F])
                act.activation(cols[:, 5:6], cols[:, 4:5], ACT.Copy, scale=SMU_S)

            @block.gpsimd
            def _(pool):
                for j in range(QUAD):
                    pool.tensor_copy(WB[:, j, j * K_ATTR:(j + 1) * K_ATTR], wf1[:])
                    pool.tensor_copy(WB[:, j, KA - 1:KA], cols[:, 3:4])
                pool.memset(pick_one[:, KA - 1:KA], 1.0).then_inc(order_p, 1)
                pool.tensor_copy(first_dst[:], DP[:, 1:2])

            @block.vector
            def _(dve):
                st = Steps(dve, order_v)
                st.did(dve.tensor_tensor(KEEP[:], DP[:, 0:T], DP[:, 1:T + 1], ALU.is_equal))
                st.did(dve.tensor_copy(iota_p[:], iota_pi[:]))
                st.did(dve.tensor_copy(iota_bf[:], iota_i[:]))
                st.did(dve.tensor_copy(SRCF[:], SRC[:, 0:T]))
                st.did(dve.tensor_copy(DSTF[:, 0:T], DP[:, 1:T + 1]))
                st.did(dve.tensor_single_scalar(LOI[:, 0:T], DP[:, 1:T + 1], P - 1, ALU.bitwise_and))
                st.did(dve.tensor_single_scalar(HII[:, 0:T], DP[:, 1:T + 1], 7, ALU.logical_shift_right))
                st.join()
                st.did(dve.tensor_copy(LOB[:, 0:T], LOI[:, 0:T]))
                st.did(dve.tensor_copy(HIB[:, 0:T], HII[:, 0:T]))
                st.did(dve.tensor_scalar(RESET[:], KEEP[:], -1.0, BIG, ALU.add, ALU.mult))
                st.did(dve.tensor_copy(seg[:, 3:4], DSTF[:, 0:1]))
                st.did(dve.tensor_copy(seg[:, 2:3], KEEP[:, 0:1]))
                st.join()
                st.did(dve.tensor_scalar(SCAT[:], DSTF[:, 0:T], seg[:, 3:4], 0.0, ALU.is_equal, ALU.add,
                                         accum_out=seg[:, 0:1]))
                st.did(dve.tensor_single_scalar(LOI[:, 0:T], SRC[:, 0:T], P - 1, ALU.bitwise_and))
                st.join()
                st.did(dve.tensor_single_scalar(seg[:, 1:2], seg[:, 0:1], float(T), ALU.is_equal))
                st.did(dve.tensor_scalar(seg[:, 3:4], iota_p[:], float(T), -1.0, ALU.mult, ALU.add))
                st.did(dve.tensor_copy(SRC_LO[:, 0:T], LOI[:, 0:T]))
                st.join()
                st.did(dve.tensor_tensor(SRC_HI[:, 0:T], SRCF[:], SRC_LO[:, 0:T], ALU.subtract))
                st.did(dve.tensor_tensor(seg[:, 3:4], seg[:, 3:4], seg[:, 0:1], ALU.add))
                st.did(dve.tensor_copy(cont_cols[:, 0, :], seg[:, 2:3].to_broadcast([P, P])))
                st.did(dve.tensor_copy(cont_cols[:, 1, :], seg[:, 1:2].to_broadcast([P, P])))
                st.join()
                dve.tensor_copy(idx_patch[:], seg[:, 3:4])
        clear()

        OH = HT.bitcast(bf16)
        ohl = OH[:, 0:2 * HALF * P].rearrange("p (h t n) -> p h t n", h=2, t=HALF)
        ohh = OH[:, 2 * HALF * P:2 * HALF * (P + NT)].rearrange("p (h t n) -> p h t n", h=2, t=HALF)
        SRC_T = TBL[:, 0:7, :].rearrange("p a b -> p (a b)").bitcast(bf16)
        srct = SRC_T[:, 0:2 * TB * P].rearrange("t (k b p) -> t k b p", k=2, b=TB)
        with nc.Block() as block:
            @block.vector
            def _(dve):
                def chunk(c, h):
                    wait(dve, counted, c - 1)
                    t = ds(c * HALF, HALF)
                    dve.tensor_tensor(ohl[:, h, :, :], iota_bf[:, :].unsqueeze(1).to_broadcast([P, HALF, P]),
                                      LOB[:, t].unsqueeze(2).to_broadcast([P, HALF, P]), ALU.is_equal)
                    dve.tensor_tensor(ohh[:, h, :, :],
                                      iota_bf[:, 0:NT].unsqueeze(1).to_broadcast([P, HALF, NT]),
                                      HIB[:, t].unsqueeze(2).to_broadcast([P, HALF, NT]),
                                      ALU.is_equal).then_inc(hot, 1)
                for h in range(2):
                    chunk(h, h)
                with dve.Fori(1, ITERS) as it:
                    for h in range(2):
                        chunk(it * 2 + h, h)
                dve.wait_ge(pe_done, 1)
                dve.tensor_copy(deg[:], bank(0)[:, 0:NT]).then_inc(cp_done, 1)
                st = Steps(dve, order_v)
                dve.wait_ge(pe_done, 2)
                le, tile, upto, last, first, has = (tmpn[:, k, :] for k in range(6))
                st.did(dve.tensor_copy(le, bank(5)[:, 0:NT]))
                st.did(dve.tensor_copy(tile, bank(5)[:, 64:64 + NT]))
                st.did(dve.tensor_copy(CONT[:], bank(6)[:, 0:P]))
                st.did(dve.tensor_copy(CHAIN_R[:], bank(6)[:, P:2 * P]))
                st.did(dve.memset(CHAIN[:], 0.0))
                st.join()
                st.then(dve.tensor_tensor_scan(upto, ones[:, 0:NT], tile, 0.0, ALU.mult, ALU.add))
                st.then(dve.tensor_tensor(upto, upto, tile, ALU.subtract))
                st.then(dve.tensor_tensor(last, upto, le, ALU.add))
                st.then(dve.tensor_tensor(first, last, deg[:], ALU.subtract))
                st.did(dve.tensor_single_scalar(last, last, -1.0, ALU.add))
                st.did(dve.tensor_single_scalar(has, deg[:], 1.0, ALU.min))
                st.join()
                for o, row in ((idx_sum, ROW_SUM), (idx_max, ROW_MAX)):
                    st.then(dve.tensor_single_scalar(le, last, -float(row), ALU.add))
                    st.then(dve.tensor_tensor(le, le, has, ALU.mult))
                    st.then(dve.tensor_single_scalar(le, le, float(row), ALU.add))
                    st.then(dve.tensor_copy(o[:], le))
                st.then(dve.tensor_single_scalar(seg[:, 3:4], iota_p[:], float(E_PAD), ALU.add))
                st.then(dve.tensor_scalar(le, first, seg[:, 3:4], None, ALU.subtract))
                st.then(dve.tensor_tensor(le, le, has, ALU.mult))
                st.then(dve.tensor_scalar(le, le, seg[:, 3:4], None, ALU.add))
                st.did(dve.tensor_copy(idx_first[:], le))
                st.did(dve.tensor_tensor(CHAIN[:, 1:P], CONT[:, 1:P], CHAIN_R[:, 0:P - 1], ALU.mult))
                st.did(dve.tensor_scalar(CONT_R[:], CONT[:], -1.0, BIG, ALU.add, ALU.mult))
                st.join()
                st.did(dve.tensor_scalar(CHAIN_R[:], CHAIN[:], -1.0, BIG, ALU.add, ALU.mult))
                dve.wait_ge(order_a, 1)
                dve.reciprocal(dinv[:], tmpn[:, 6, :])

            @block.tensor
            def _(pe):
                def chunk(c, h, first=False, last=False):
                    pe.wait_ge(hot, c + 1)
                    for j in range(HALF):
                        m = nc.tensor.matmul(bank(0)[:, 0:NT], ohl[:, h, j, :], ohh[:, h, j, :],
                                             start=first and j == 0, stop=last and j == HALF - 1,
                                             skip_group_check=True)
                    m.then_inc(counted, 1)
                for h in range(2):
                    chunk(h, h, first=h == 0)
                with pe.Fori(1, ITERS - 1) as it:
                    for h in range(2):
                        chunk(it * 2 + h, h)
                for h in range(2):
                    chunk(2 * ITERS - 2 + h, h, last=h == 1)
                for k in range(2 * TB):
                    which, b = divmod(k, TB)
                    w = min(P, T - b * P)
                    wait(pe, turned_sb, k - 3)
                    nc.tensor.transpose(bank(1 + k % 4)[0:w, 0:P],
                                        (SRC_HI, SRC_LO)[which][:, b * P:b * P + w],
                                        ident[:]).then_inc(turned, 1)
                    if k == 0:
                        pe.wait_ge(counted, 2 * ITERS)
                        nc.tensor.matmul(bank(7)[0:1, 0:1], ident[:, 0:1], ones[:, 0:1], start=True,
                                         stop=True).then_inc(pe_done, 1)
                pe.wait_ge(cp_done, 1)
                nc.tensor.matmul(bank(5)[:, 0:NT], upper[:], deg[:], start=True, stop=True)
                nc.tensor.matmul(bank(5)[:, 64:64 + NT], ones[:], deg[:], start=True, stop=True)
                nc.tensor.matmul(bank(6)[:, 0:P], cont_cols[:, 0, :], ident[:], start=True, stop=True)
                nc.tensor.matmul(bank(6)[:, P:2 * P], cont_cols[:, 1, :], ident[:], start=True,
                                 stop=True).then_inc(pe_done, 1)

            @block.scalar
            def _(act):
                for k in range(2 * TB):
                    which, b = divmod(k, TB)
                    w = min(P, T - b * P)
                    act.wait_ge(turned, k + 1)
                    act.copy(srct[0:w, which, b, :], bank(1 + k % 4)[0:w, 0:P]).then_inc(turned_sb, 1)
                act.wait_ge(cp_done, 1)
                act.activation(tmpn[:, 6, :], deg[:], ACT.Sqrt, bias=ones[:, 0:1]).then_inc(order_a, 1)

            @block.sync
            def _(sp):
                sp.dma_start(run_rows[ROW_SUM:ROW_SUM + 1, :], zeros[0:1, 0:F]).then_inc(table_out, 16)
                sp.dma_start(run_rows[ROW_MAX:ROW_MAX + 1, :], neutral[0:1, :]).then_inc(table_out, 16)
                n = 32
                sp.wait_ge(turned_sb, 2 * TB)
                for k in range(2):
                    rows = src_rows[k, :].rearrange("(t p) -> t p", p=P)
                    full = T // P
                    sp.dma_start(rows[0:full * P, :].rearrange("(b t) p -> t b p", t=P),
                                 srct[:, k, 0:full, :]).then_inc(table_out, 16)
                    sp.dma_start(rows[full * P:T, :], srct[0:T - full * P, k, full, :])\
                        .then_inc(table_out, 16)
                    n += 32
                sp.wait_ge(table_out, n)
        clear()

        def group_rows(ap, g):
            return ap[g * GN:(g + 1) * GN, :].rearrange("(t p) f -> p t f", p=P)

        def tile_cols(g, t):
            return g * GROUP + t

        def node_phase(index, layer_count, post, norm_x, weight, width, finish, scatter=False):
            base = [total.rows[s] + layer_count * 16 * GROUP * len(range(s, NG, 2)) for s in range(2)]
            banks_m = lambda t: bank(2 + t // (512 // width))[:, t % (512 // width) * width:
                                                              (t % (512 // width) + 1) * width]
            with nc.Block() as block:
                if index is not None or scatter:
                    @block.gpsimd
                    def _(pool):
                        for g in range(NG):
                            s = g % 2
                            if index is not None:
                                wait(pool, rows_used, g - 1)
                                for t in range(GROUP):
                                    k = tile_cols(g, t)
                                    pool.indirect_dma_start(
                                        NR[:, s, t, :], None, run_rows,
                                        bass.IndirectOffsetOnAxis(index[:, k:k + 1].bitcast(u32), 0))\
                                        .then_inc(rows_landed[s], 16)
                        if scatter:
                            for g in range(NG):
                                pool.wait_ge(table_ready, g + 1)
                                for t in range(GROUP):
                                    k = tile_cols(g, t)
                                    pool.indirect_dma_start(
                                        fill_rows, bass.IndirectOffsetOnAxis(idx_first[:, k:k + 1].bitcast(u32), 0),
                                        TBL[:, k, :], None).then_inc(firsts, 16)
                            pool.wait_ge(firsts, 16 * NT)

                @block.vector
                def _(dve):
                    st = Steps(dve, order_v)

                    def front(g):
                        s = g % 2
                        if index is not None:
                            dve.wait_ge(rows_landed[s], base[s] + 16 * GROUP * (g // 2 + 1))
                        if not norm_x:
                            wait(dve, turned, g - 1)
                        if post is not None:
                            last = post(dve, st, g, s)
                            last.then_inc(rows_used, 1)
                            if not norm_x:
                                last2 = dve.wait_ge(rows_used, g + 1)
                        if norm_x:
                            if post is not None:
                                dve.wait_ge(rows_used, g + 1)
                            for t in range(GROUP):
                                st.did(dve.bn_stats(stats[:, t, :], X[:, tile_cols(g, t), :]))
                            st.join()
                            for t in range(GROUP):
                                i = dve.bn_aggr(mv[:, s, t, :], stats[:, t, :])
                            wait(dve, feat_ready, g - 1)
                            i = st.did(i)
                            st.join()
                            st.then(dve.tensor_single_scalar(norm[:, s, 0, :], mv[:, s, :, 1], EPS, ALU.add))
                            dve.sem_inc(var_ready, 1)
                            dve.wait_ge(std_ready, g + 1)
                            st.then(dve.reciprocal(norm[:, s, 1, :], norm[:, s, 0, :]))
                            dve.scalar_tensor_tensor(norm[:, s, 2, :], mv[:, s, :, 0], -1.0, norm[:, s, 1, :],
                                                     ALU.mult, ALU.mult).then_inc(norm_ready, 1)

                    def back(g):
                        dve.wait_ge(projected, g + 1)
                        finish(dve, st, g, banks_m).then_inc(table_ready, 1)

                    for g in range(NG + 1):
                        if g < NG:
                            front(g)
                        if g > 0:
                            back(g - 1)

                @block.scalar
                def _(act):
                    def front(g):
                        s = g % 2
                        act.wait_ge(var_ready, g + 1)
                        act.activation(norm[:, s, 0, :], norm[:, s, 0, :], ACT.Sqrt).then_inc(std_ready, 1)
                        act.wait_ge(norm_ready, g + 1)
                        wait(act, turned, g - 1)
                        for t in range(GROUP):
                            i = act.activation(FE[:, s, t, :], X[:, tile_cols(g, t), :], ACT.Relu,
                                               bias=norm[:, s, 2, t:t + 1], scale=norm[:, s, 1, t:t + 1])
                        i.then_inc(feat_ready, 1)

                    def turn(g):
                        s = g % 2
                        act.wait_ge(turned, g + 1)
                        wait(act, projected, g - 1)
                        act.copy(FT[:, s, 0:512], bank(0))
                        act.copy(FT[:, s, 512:GN], bank(1)[:, 0:GN - 512]).then_inc(turned_sb, 1)

                    for g in range(NG + 1):
                        if norm_x and g < NG:
                            front(g)
                        if g > 0:
                            turn(g - 1)

                @block.tensor
                def _(pe):
                    for g in range(NG):
                        s = g % 2
                        if norm_x:
                            pe.wait_ge(feat_ready, g + 1)
                        else:
                            pe.wait_ge(rows_used, g + 1)
                        wait(pe, turned_sb, g)
                        for t in range(GROUP):
                            m = nc.tensor.transpose(bank(t // 4)[:, t % 4 * P:(t % 4 + 1) * P],
                                                    FE[:, s, t, :], ident[:])
                        m.then_inc(turned, 1)
                        pe.wait_ge(turned_sb, g + 1)
                        wait(pe, table_ready, g)
                        for t in range(GROUP):
                            m = nc.tensor.matmul(banks_m(t), FT[:, s, t * P:(t + 1) * P], weight,
                                                 start=True, stop=True)
                        m.then_inc(projected, 1)

                @block.sync
                def _(sp):
                    for g in range(NG):
                        sp.wait_ge(table_ready, g + 1)
                        sp.dma_start(group_rows(table, g), TBL[:, g * GROUP:(g + 1) * GROUP, :])\
                            .then_inc(table_out, 16)
                    sp.wait_ge(table_out, 16 * NG)
            clear()

        def rows_gathered(times=1):
            for s in range(2):
                total.rows[s] += times * 16 * GROUP * len(range(s, NG, 2))

        def gsl(g):
            return slice(g * GROUP, (g + 1) * GROUP)

        def per_node(g):
            return dinv[:, gsl(g)].unsqueeze(2).to_broadcast([P, GROUP, F])

        with nc.Block() as block:
            @block.vector
            def _(dve):
                st = Steps(dve, order_v)
                for g in range(NG):
                    s = g % 2
                    for t in range(GROUP):
                        st.did(dve.bn_stats(stats[:, t, :], X[:, tile_cols(g, t), :]))
                    st.join()
                    wait(dve, feat_ready, g - 1)
                    for t in range(GROUP):
                        st.did(dve.bn_aggr(mv[:, s, t, :], stats[:, t, :]))
                    st.join()
                    dve.tensor_single_scalar(norm[:, s, 0, :], mv[:, s, :, 1], EPS, ALU.add)\
                        .then_inc(var_ready, 1)
                    dve.wait_ge(std_ready, g + 1)
                    st.then(dve.reciprocal(norm[:, s, 1, :], norm[:, s, 0, :]))
                    dve.scalar_tensor_tensor(norm[:, s, 2, :], mv[:, s, :, 0], -1.0, norm[:, s, 1, :],
                                             ALU.mult, ALU.mult).then_inc(norm_ready, 1)
                for g in range(NG):
                    dve.wait_ge(evicted, g + 1)
                    for k in range(2):
                        lo = g * GN + k * (GN // 2)
                        hi = min(lo + GN // 2, N)
                        st.did(dve.bn_stats(stats[:, 2 * g + k, :], HT[:, lo:hi]))
                st.join()
                st.then(dve.bn_aggr(bnp[:, 0:2], stats[:, :, :].rearrange("p a b -> p (a b)")))
                st.then(dve.tensor_single_scalar(bnp[:, 2:3], bnp[:, 1:2], EPS, ALU.add))
                dve.sem_inc(pe_done, 1)
                dve.wait_ge(cp_done, 1)
                st.then(dve.reciprocal(bnp[:, 3:4], bnp[:, 2:3]))
                st.then(dve.tensor_tensor(bnp[:, 4:5], bnp[:, 3:4], cols[:, 1:2], ALU.mult))
                st.then(dve.tensor_tensor(bnp[:, 5:6], bnp[:, 0:1], bnp[:, 4:5], ALU.mult))
                st.then(dve.tensor_tensor(bnp[:, 6:7], cols[:, 2:3], bnp[:, 5:6], ALU.subtract))
                dve.sem_inc(compared, 1)
                for g in range(NG):
                    dve.wait_ge(projected, NG + g + 1)
                    for h in range(2):
                        t = slice(0, 4) if h == 0 else slice(4, GROUP)
                        n = t.stop - t.start
                        k = slice(g * GROUP + t.start, g * GROUP + t.stop)
                        i = dve.tensor_tensor(TBL[:, k, :],
                                              bank(2 * (g % 2) + h)[:, 0:n * P].rearrange("p (t f) -> p t f", f=F),
                                              dinv[:, k].unsqueeze(2).to_broadcast([P, n, F]), ALU.mult)
                    i.then_inc(table_ready, 1)

            @block.scalar
            def _(act):
                for g in range(NG):
                    s = g % 2
                    act.wait_ge(var_ready, g + 1)
                    act.activation(norm[:, s, 0, :], norm[:, s, 0, :], ACT.Sqrt).then_inc(std_ready, 1)
                    act.wait_ge(norm_ready, g + 1)
                    wait(act, turned, g - 1)
                    for t in range(GROUP):
                        i = act.activation(FE[:, s, t, :], X[:, tile_cols(g, t), :], ACT.Relu,
                                           bias=norm[:, s, 2, t:t + 1], scale=norm[:, s, 1, t:t + 1])
                    i.then_inc(feat_ready, 1)
                    act.wait_ge(turned, g + 1)
                    wait(act, projected, g - 1)
                    act.copy(FT[:, s, 0:512], bank(0))
                    act.copy(FT[:, s, 512:GN], bank(1)[:, 0:GN - 512]).then_inc(turned_sb, 1)
                    act.wait_ge(projected, g + 1)
                    act.activation(HT[:, g * GN:g * GN + 512], bank(2), ACT.Identity, bias=cols[:, 0:1])
                    act.activation(HT[:, g * GN + 512:(g + 1) * GN], bank(3)[:, 0:GN - 512], ACT.Identity,
                                   bias=cols[:, 0:1]).then_inc(evicted, 1)
                act.wait_ge(pe_done, 1)
                act.activation(bnp[:, 2:3], bnp[:, 2:3], ACT.Sqrt).then_inc(cp_done, 1)
                act.wait_ge(compared, 1)
                for g in range(NG):
                    h = HT[:, g * GN:(g + 1) * GN]
                    act.activation(h, h, ACT.Identity, bias=bnp[:, 6:7], scale=bnp[:, 4:5]).then_inc(attr_sb, 1)

            @block.tensor
            def _(pe):
                for g in range(NG):
                    s = g % 2
                    pe.wait_ge(feat_ready, g + 1)
                    wait(pe, turned_sb, g)
                    for t in range(GROUP):
                        m = nc.tensor.transpose(bank(t // 4)[:, t % 4 * P:(t % 4 + 1) * P], FE[:, s, t, :],
                                                ident[:])
                    m.then_inc(turned, 1)
                    pe.wait_ge(turned_sb, g + 1)
                    wait(pe, evicted, g)
                    nc.tensor.matmul(bank(2), WT[:, 0, :], FT[:, s, 0:512], start=True, stop=True)
                    nc.tensor.matmul(bank(3)[:, 0:GN - 512], WT[:, 0, :], FT[:, s, 512:GN], start=True,
                                     stop=True).then_inc(projected, 1)
                for g in range(NG):
                    pe.wait_ge(attr_sb, g + 1)
                    wait(pe, table_ready, g - 1)
                    for t in range(GROUP):
                        m = nc.tensor.transpose(bank(2 * (g % 2) + t // 4)[:, t % 4 * P:(t % 4 + 1) * P],
                                                HT[:, g * GN + t * P:g * GN + (t + 1) * P], ident[:])
                    m.then_inc(projected, 1)

            @block.sync
            def _(sp):
                for g in range(NG):
                    sp.wait_ge(table_ready, g + 1)
                    sp.dma_start(group_rows(table, g), TBL[:, gsl(g), :]).then_inc(table_out, 16)
                sp.wait_ge(table_out, 16 * NG)
        clear()

        def edge_pass(maximum, layer=0, leaders=False):
            base = total.gathers + layer * (16 * T // RING)
            scale = RESET if maximum else KEEP
            op0, op1 = (ALU.add, ALU.max) if maximum else (ALU.mult, ALU.add)
            with nc.Block() as block:
                @block.gpsimd
                def _(pool):
                    def body(it):
                        for j in range(UNROLL):
                            h, s = j // HALF, j % RING
                            if j % HALF == 0:
                                hold(pool, staged, it * 2 + h + 1)
                            n = it * UNROLL + j - RING + 1
                            hold(pool, reduced, n)
                            pool.indirect_dma_start(
                                G[:, s, :], None, table,
                                bass.IndirectOffsetOnAxis(stage[:, h, j % HALF:j % HALF + 1].bitcast(u32), 0))\
                                .then_inc(landed[s], 16)
                    body(0)
                    with pool.Fori(1, ITERS) as it:
                        body(it)

                @block.scalar
                def _(act):
                    def body(it):
                        for h in range(2):
                            wait(act, reduced, (it * 2 + h - 1) * HALF)
                            act.copy(stage[:, h, :], SRCF[:, ds(it * UNROLL + h * HALF, HALF)])\
                                .then_inc(staged, 1)
                    body(0)
                    if leaders:
                        flat = attr_pad.rearrange("e k -> (e k)")
                        act.dma_start(flat[0:E * K_ATTR].rearrange("(a b) -> a b", a=50),
                                     edge_attr.rearrange("e k -> (e k)").rearrange("(a b) -> a b", a=50))\
                            .then_inc(table_out, 16)
                        left = E_PAD - E
                        act.dma_start(attr_pad[E:E + P, :], zeros[:, 0:K_ATTR]).then_inc(table_out, 16)
                        act.dma_start(attr_pad[E + P:E_PAD, :], zeros[0:left - P, 0:K_ATTR])\
                            .then_inc(table_out, 16)
                        for k in range(ACCS):
                            rows = acc_dram[k].rearrange("(p t) f -> p (t f)", p=P)
                            for c in range(0, (NT + 1) * F, HALF * F):
                                w = min(HALF * F, (NT + 1) * F - c)
                                act.dma_start(rows[:, c:c + w], zeros[:, 0:w]).then_inc(table_out, 16)
                    with act.Fori(1, ITERS) as it:
                        body(it)
                    if leaders:
                        act.wait_ge(table_out, 16 * (3 + ACCS * -(-(NT + 1) // HALF)))

                @block.vector
                def _(dve):
                    dve.memset(RUN[:, 1, HALF - 1, :], -BIG if maximum else 0.0).then_inc(order_v, 1)
                    dve.wait_ge(order_v, 1)

                    def body(it):
                        for j in range(UNROLL):
                            h, k, s = j // HALF, j % HALF, j % RING
                            t = it * UNROLL + j
                            if k == 0:
                                wait(dve, stored[h], it * 16)
                            dve.wait_ge(landed[s], base + it * (16 * UNROLL // RING) + 16 * (j // RING + 1))
                            wait(dve, reduced, t)
                            hp, kp = (h, k - 1) if k else (1 - h, HALF - 1)
                            dve.scalar_tensor_tensor(RUN[:, h, k, :], RUN[:, hp, kp, :], scale[:, ds(t, 1)],
                                                     G[:, s, :], op0, op1).then_inc(reduced, 1)
                            if leaders:
                                if j % QUAD == 0:
                                    dve.wait_ge(spread, it * (UNROLL // QUAD) + j // QUAD + 1)
                                    wait(dve, compared, t)
                                dve.scalar_tensor_tensor(
                                    SAME[:, 0, j % QUAD, :],
                                    bank(j // QUAD % 2)[:, j % QUAD * P:(j % QUAD + 1) * P],
                                    SRCF[:, ds(t, 1)], lower[:], ALU.is_equal, ALU.mult,
                                    accum_out=SCAT[:, ds(t, 1)]).then_inc(compared, 1)
                    body(0)
                    with dve.Fori(1, ITERS) as it:
                        body(it)

                if leaders:
                    @block.tensor
                    def _(pe):
                        def body(it):
                            for q in range(UNROLL // QUAD):
                                h, k = q // CQ, q % CQ
                                if k == 0:
                                    pe.wait_ge(rows_in[h], it * 16 + 16)
                                wait(pe, compared, it * UNROLL + (q - 1) * QUAD)
                                nc.tensor.matmul(bank(q % 2), ones_bf[:],
                                                 SROW[:, h, k * QUAD * P:(k + 1) * QUAD * P],
                                                 start=True, stop=True).then_inc(spread, 1)
                        body(0)
                        with pe.Fori(1, ITERS) as it:
                            body(it)

                @block.sync
                def _(sp):
                    def body(it):
                        for h in range(2):
                            c = it * 2 + h
                            if leaders:
                                hold(sp, spread, (c - 1) * CQ)
                                sp.dma_start(SROW[:, h, :], src_rows[:, ds(c * HALF * P, HALF * P)])\
                                    .then_inc(rows_in[h], 16)
                                hold(sp, zeroed[h], it * 16)
                                sp.dma_start(fill_view[:, ds(c * HALF * F, HALF * F)], zeros[:])\
                                    .then_inc(zeroed[h], 16)
                            hold(sp, reduced, (c + 1) * HALF)
                            sp.dma_start(run_view[:, ds(c * HALF * F, HALF * F)],
                                         RUN[:, h, :, :].rearrange("p t f -> p (t f)"))\
                                .then_inc(stored[h], 16)
                    body(0)
                    with sp.Fori(1, ITERS) as it:
                        body(it)
                    for h in range(2):
                        sp.wait_ge(stored[h], 16 * ITERS)
                        if leaders:
                            sp.wait_ge(zeroed[h], 16 * ITERS)
            clear()

            pbase = total.patches + layer * 32
            with nc.Block() as block:
                @block.tensor
                def _(pe):
                    nc.tensor.transpose(bank(0)[:, 0:P], RUN[:, 1, HALF - 1, :], ident[:]).then_inc(pe_done, 1)
                    pe.wait_ge(cp_done, 1)
                    nc.tensor.transpose(bank(1)[:, 0:P], carry_t[:, 1, :], ident[:]).then_inc(pe_done, 1)

                @block.vector
                def _(dve):
                    st = Steps(dve, order_v)
                    st.then(dve.memset(carry_t[:, 0, :], -BIG if maximum else 0.0))
                    dve.wait_ge(pe_done, 1)
                    st.then(dve.tensor_tensor(carry_t[:, 0, 1:P], bank(0)[:, 0:P - 1],
                                              (CONT_R if maximum else CONT)[:, 1:P],
                                              ALU.add if maximum else ALU.mult))
                    dve.tensor_tensor_scan(carry_t[:, 1, :], (CHAIN_R if maximum else CHAIN)[:],
                                           carry_t[:, 0, :], -BIG if maximum else 0.0, op0, op1)\
                        .then_inc(cp_done, 1)
                    dve.wait_ge(pe_done, 2)
                    dve.wait_ge(patched, pbase + 16)
                    dve.tensor_tensor(patch[:, 1, :], patch[:, 0, :], bank(1)[:, 0:P], op1)\
                        .then_inc(cp_done, 1)
                    if leaders:
                        st.then(dve.tensor_single_scalar(seg[:, 3:4], iota_p[:], float(N_PAD), ALU.add))
                        st.did(dve.tensor_single_scalar(SCAT[:], SCAT[:], 1.0, ALU.is_equal))
                        st.did(dve.tensor_scalar(FILL[:, 0, 0:7, :].rearrange("p a b -> p (a b)")[:, 0:T],
                                                 SRCF[:], seg[:, 3:4], None, ALU.subtract))
                        st.join()
                        st.then(dve.tensor_tensor(SCAT[:], SCAT[:],
                                                  FILL[:, 0, 0:7, :].rearrange("p a b -> p (a b)")[:, 0:T],
                                                  ALU.mult))
                        st.then(dve.tensor_scalar(SCAT[:], SCAT[:], seg[:, 3:4], None, ALU.add))

                @block.gpsimd
                def _(pool):
                    at = bass.IndirectOffsetOnAxis(idx_patch[:].bitcast(u32), 0)
                    pool.indirect_dma_start(patch[:, 0, :], None, run_rows, at).then_inc(patched, 16)
                    pool.wait_ge(cp_done, 2)
                    pool.indirect_dma_start(run_rows, at, patch[:, 1, :], None).then_inc(patched, 16)
                    hold(pool, patched, pbase + 32)
            clear()

        def passed(times=1):
            total.gathers += times * (16 * T // RING)
            total.patches += times * 32

        edge_pass(False, leaders=True)
        passed()

        def post_gcn(bias):
            def post(dve, st, g, s):
                rows = NR[:, s, :, :]
                st.then(dve.tensor_tensor(rows, rows, TBL[:, gsl(g), :], ALU.add))
                st.then(dve.tensor_tensor(rows, rows, per_node(g), ALU.mult))
                if bias is None:
                    return dve.scalar_tensor_tensor(X[:, gsl(g), :], rows, 0.0, X[:, gsl(g), :],
                                                    ALU.max, ALU.add)
                return dve.tensor_tensor(FE[:, s, :, :], rows,
                                         bias_g[:, bias, :].unsqueeze(1).to_broadcast([P, GROUP, F]), ALU.add)
            return post

        def by_bank(g, banks_m, width, ap):
            per = 512 // width
            for t in range(0, GROUP, per):
                n = min(per, GROUP - t)
                yield t, n, bank(2 + t // per)[:, 0:n * width].rearrange("p (t f) -> p t f", f=width)

        def finish_plain(dve, st, g, banks_m):
            for t, n, ps in by_bank(g, banks_m, F, None):
                i = dve.tensor_copy(TBL[:, g * GROUP + t:g * GROUP + t + n, :], ps)
            return i

        def finish_gcn(dve, st, g, banks_m):
            for t, n, ps in by_bank(g, banks_m, F, None):
                k = slice(g * GROUP + t, g * GROUP + t + n)
                i = dve.tensor_tensor(TBL[:, k, :], ps, dinv[:, k].unsqueeze(2).to_broadcast([P, n, F]), ALU.mult)
            return i

        def finish_edgeconv(bias):
            def finish(dve, st, g, banks_m):
                parts = list(by_bank(g, banks_m, 2 * F, None))
                for t, n, ps in parts:
                    k = slice(g * GROUP + t, g * GROUP + t + n)
                    st.did(dve.tensor_copy(TBL[:, k, :], ps[:, :, 0:F]))
                st.join()
                for t, n, ps in parts:
                    k = slice(g * GROUP + t, g * GROUP + t + n)
                    st.did(dve.tensor_tensor(BASE[:, k, :], ps[:, :, F:2 * F], TBL[:, k, :], ALU.subtract))
                st.join()
                return dve.tensor_tensor(BASE[:, gsl(g), :], BASE[:, gsl(g), :],
                                         bias.unsqueeze(1).to_broadcast([P, GROUP, F]), ALU.add)
            return finish

        node_phase(idx_sum, 0, post_gcn(None), True, WT[:, 1, :], F, finish_plain, scatter=True)
        rows_gathered()

        QI = UNROLL // QUAD
        attr_view = attr_pad.rearrange("(p t) k -> p (t k)", t=T)
        with nc.Block() as block:
            @block.gpsimd
            def _(pool):
                pool.indirect_dma_start(HX[:, 2 * QUAD - 1, :], None, table,
                                        bass.IndirectOffsetOnAxis(first_dst[:].bitcast(u32), 0))\
                    .then_inc(patched, 16)

                def body(it):
                    for j in range(UNROLL):
                        h, a = j // HALF, j % ACCS
                        if j % HALF == 0:
                            hold(pool, staged, it * 2 + h + 1)
                        n = it * (16 * UNROLL // ACCS) + 16 * (j // ACCS)
                        hold(pool, added[a], n)
                        if j % QUAD == 0:
                            hold(pool, totalled, it * QI + j // QUAD + 1)
                        pool.indirect_dma_start(
                            acc_dram[a],
                            bass.IndirectOffsetOnAxis(stage[:, h, j % HALF:j % HALF + 1].bitcast(u32), 0),
                            TOT[:, j // QUAD % 2, a * F:(a + 1) * F], None, compute_op=ALU.add).then_inc(added[a], 16)
                body(0)
                with pool.Fori(1, ITERS) as it:
                    body(it)
                for a in range(ACCS):
                    pool.wait_ge(added[a], 16 * (T // ACCS))

            @block.sync
            def _(sp):
                def body(it):
                    for h in range(2):
                        c = it * 2 + h
                        hold(sp, attr_turned, (c - 1) * CQ)
                        sp.dma_start(AT[:, h, :, 0:KA - 1],
                                     attr_view[:, ds(c * HALF * K_ATTR, HALF * K_ATTR)]
                                     .rearrange("p (q k) -> p q k", q=CQ)).then_inc(attr_in[h], 16)
                        hold(sp, spread, (c - 1) * CQ)
                        sp.dma_start(SROW[:, h, :], src_rows[:, ds(c * HALF * P, HALF * P)])\
                            .then_inc(rows_in[h], 16)
                        hold(sp, expanded, (c - 1) * HALF)
                        sp.dma_start(FILL[:, h, :, :].rearrange("p t f -> p (t f)"),
                                     fill_view[:, ds(c * HALF * F, HALF * F)]).then_inc(fill_in[h], 16)
                body(0)
                with sp.Fori(1, ITERS) as it:
                    body(it)

            @block.tensor
            def _(pe):
                def turn(it, q):
                    n, q = it * QI + q, q % (2 * QI)
                    h, k = q // CQ % 2, q % CQ
                    if k == 0:
                        pe.wait_ge(attr_in[h], (it + q // QI) * 16 + 16)
                    wait(pe, attr_sb, n)
                    nc.tensor.transpose(bank(0)[0:KA, 0:P], AT[:, h, k, :], ident[:])\
                        .then_inc(attr_turned, 1)

                def spread_src(it, q):
                    n, q = it * QI + q, q % (2 * QI)
                    h, k = q // CQ % 2, q % CQ
                    if k == 0:
                        pe.wait_ge(rows_in[h], (it + q // QI) * 16 + 16)
                    wait(pe, compared, (n - 1) * QUAD)
                    nc.tensor.matmul(bank(6 + q % 2), ones_bf[:], SROW[:, h, k * QUAD * P:(k + 1) * QUAD * P],
                                     start=True, stop=True).then_inc(spread, 1)

                def hide(it, q):
                    n = it * QI + q
                    pe.wait_ge(attr_sb, n + 1)
                    wait(pe, gelu_done, n - 1)
                    for j in range(QUAD):
                        m = nc.tensor.matmul(bank(2 + q % 2)[:, j * P:(j + 1) * P], W1Q[:, j, :],
                                             ATT[:, q % 4, :], start=True, stop=True)
                    m.then_inc(hidden, 1)

                def filters(it, q):
                    n = it * QI + q
                    pe.wait_ge(gelu_done, n + 1)
                    wait(pe, messaged, (n - 1) * QUAD)
                    for j in range(QUAD):
                        o = bank(4 + q % 2)[:, j * F:(j + 1) * F]
                        nc.tensor.matmul(o, GH[:, q % 2, j * P:(j + 1) * P], WF2G[:], start=True, stop=False)
                        m = nc.tensor.matmul(o, ATT[:, q % 4, :], W21Q[:, j, :], start=False, stop=True)
                    m.then_inc(filtered, 1)

                def sum_same(it, q):
                    n = it * QI + q
                    pe.wait_ge(compared, (n + 1) * QUAD)
                    pe.wait_ge(messaged, (n + 1) * QUAD)
                    wait(pe, totalled, n)
                    for j in range(QUAD):
                        m = nc.tensor.matmul(bank(1)[:, j * F:(j + 1) * F], SAME[:, q % 4, j, :],
                                             MSG[:, q % 2, j, :], start=True, stop=True)
                    m.then_inc(summed, 1)

                def body(it, first=False, last=False):
                    for q in range(QI):
                        if not last or q + 2 < QI:
                            turn(it, q + 2)
                            spread_src(it, q + 2)
                        if not last or q + 1 < QI:
                            hide(it, q + 1)
                        filters(it, q)
                        if not first or q > 0:
                            if q > 0:
                                sum_same(it, q - 1)
                            else:
                                sum_same(it - 1, QI - 1)
                turn(0, 0)
                turn(0, 1)
                spread_src(0, 0)
                spread_src(0, 1)
                hide(0, 0)
                body(0, first=True)
                with pe.Fori(1, ITERS - 1) as it:
                    body(it)
                body(ITERS - 1, last=True)
                sum_same(ITERS - 1, QI - 1)

            @block.scalar
            def _(act):
                def copy_attr(it, q):
                    n = it * QI + q
                    act.wait_ge(attr_turned, n + 1)
                    wait(act, filtered, n - 3)
                    act.copy(ATT[:, q % 4, :], bank(0)[0:KA, 0:P]).then_inc(attr_sb, 1)

                def gelu(it, q):
                    n = it * QI + q
                    act.wait_ge(hidden, n + 1)
                    wait(act, filtered, n - 1)
                    act.activation(GH[:, q % 2, :], bank(2 + q % 2), ACT.Gelu, scale=SMU_S)\
                        .then_inc(gelu_done, 1)

                def copy_totals(it, q):
                    n = it * QI + q
                    act.wait_ge(summed, n + 1)
                    for a in range(ACCS):
                        wait(act, added[a], (n - 1) * 16)
                    act.copy(TOT[:, q % 2, :], bank(1)).then_inc(totalled, 1)

                def body(it, first=False, last=False):
                    for q in range(QI):
                        if q % CQ == 0:
                            h = q // CQ
                            for a in range(ACCS):
                                wait(act, added[a], (it * 2 + h - 1) * (16 * HALF // ACCS))
                            act.copy(stage[:, h, :], SCAT[:, ds(it * UNROLL + h * HALF, HALF)])\
                                .then_inc(staged, 1)
                        if not last or q + 2 < QI:
                            copy_attr(it, q + 2)
                        if not last or q + 1 < QI:
                            gelu(it, q + 1)
                        if not first or q > 0:
                            if q > 0:
                                copy_totals(it, q - 1)
                            else:
                                copy_totals(it - 1, QI - 1)
                copy_attr(0, 0)
                copy_attr(0, 1)
                gelu(0, 0)
                body(0, first=True)
                with act.Fori(1, ITERS - 1) as it:
                    body(it)
                body(ITERS - 1, last=True)
                copy_totals(ITERS - 1, QI - 1)

            @block.vector
            def _(dve):
                dve.wait_ge(patched, total.patches + 16)

                def expand(it, q):
                    n = it * QI + q
                    h = q // CQ % 2
                    for j in range(QUAD):
                        t, k, s = n * QUAD + j, q % CQ * QUAD + j, q % 2 * QUAD + j
                        if k == 0:
                            dve.wait_ge(fill_in[h], (it + q // QI) * 16 + 16)
                        wait(dve, messaged, t - 2 * QUAD + 1)
                        wait(dve, expanded, t)
                        dve.scalar_tensor_tensor(HX[:, s, :], HX[:, s - 1 if s else 2 * QUAD - 1, :],
                                                 KEEP[:, ds(t, 1)], FILL[:, h, k, :], ALU.mult, ALU.add)\
                            .then_inc(expanded, 1)
                        if j == 0:
                            dve.wait_ge(spread, n + 1)
                            wait(dve, summed, n - 3)
                        dve.scalar_tensor_tensor(SAME[:, q % 4, j, :],
                                                 bank(6 + q % 2)[:, j * P:(j + 1) * P], SRCF[:, ds(t, 1)],
                                                 lower[:], ALU.is_equal, ALU.mult).then_inc(compared, 1)

                def message(it, q):
                    n = it * QI + q
                    dve.wait_ge(filtered, n + 1)
                    wait(dve, summed, n - 1)
                    dve.wait_ge(expanded, (n + 1) * QUAD)
                    for j in range(QUAD):
                        dve.scalar_tensor_tensor(MSG[:, q % 2, j, :],
                                                 bank(4 + q % 2)[:, j * F:(j + 1) * F],
                                                 WEIGHT[:, ds(n * QUAD + j, 1)], HX[:, q % 2 * QUAD + j, :],
                                                 ALU.mult, ALU.mult).then_inc(messaged, 1)

                def body(it, last=False):
                    for q in range(QI):
                        if not last or q + 1 < QI:
                            expand(it, q + 1)
                        message(it, q)
                expand(0, 0)
                body(0)
                with dve.Fori(1, ITERS - 1) as it:
                    body(it)
                body(ITERS - 1, last=True)
        clear()
        total.patches += 16

        with nc.Block() as block:
            @block.sync
            def _(sp):
                for g in range(NG):
                    s = g % 2
                    wait(sp, rows_used, g - 1)
                    for k in range(ACCS):
                        sp.dma_start(ACC[:, s, k, :, :], group_rows(acc_dram[k], g)).then_inc(acc_in[s], 16)

            @block.vector
            def _(dve):
                st = Steps(dve, order_v)
                for g in range(NG + 1):
                    if g < NG:
                        s = g % 2
                        dve.wait_ge(acc_in[s], 16 * ACCS * (g // 2 + 1))
                        st.did(dve.tensor_tensor(ACC[:, s, 0, :, :], ACC[:, s, 0, :, :], ACC[:, s, 1, :, :],
                                                 ALU.add))
                        st.did(dve.tensor_tensor(ACC[:, s, 2, :, :], ACC[:, s, 2, :, :], ACC[:, s, 3, :, :],
                                                 ALU.add))
                        st.join()
                        wait(dve, projected, g - 1)
                        dve.tensor_tensor(FE[:, s, :, :], ACC[:, s, 0, :, :], ACC[:, s, 2, :, :], ALU.add)\
                            .then_inc(rows_used, 1)
                    if g > 0:
                        dve.wait_ge(projected, g)
                        for t, n in ((0, 4), (4, GROUP - 4)):
                            k = slice((g - 1) * GROUP + t, (g - 1) * GROUP + t + n)
                            i = dve.tensor_tensor(X[:, k, :], X[:, k, :],
                                                  bank(4 + t // 4)[:, 0:n * F].rearrange("p (t f) -> p t f", f=F),
                                                  ALU.add)
                        st.did(i)
                        st.join()
                        dve.tensor_tensor(X[:, gsl(g - 1), :], X[:, gsl(g - 1), :],
                                          bias_o2[:, :].unsqueeze(1).to_broadcast([P, GROUP, F]), ALU.add)\
                            .then_inc(evicted, 1)

            @block.tensor
            def _(pe):
                for g in range(NG):
                    s = g % 2
                    pe.wait_ge(rows_used, g + 1)
                    wait(pe, turned_sb, g)
                    for t in range(GROUP):
                        m = nc.tensor.transpose(bank(t // 4)[:, t % 4 * P:(t % 4 + 1) * P], FE[:, s, t, :],
                                                ident[:])
                    m.then_inc(turned, 1)
                    pe.wait_ge(turned_sb, g + 1)
                    wait(pe, gelu_done, g)
                    nc.tensor.matmul(bank(2), WO1[:], FT[:, s, 0:512], start=True, stop=True)
                    nc.tensor.matmul(bank(3)[:, 0:GN - 512], WO1[:], FT[:, s, 512:GN], start=True, stop=True)\
                        .then_inc(hidden, 1)
                    pe.wait_ge(gelu_done, g + 1)
                    wait(pe, evicted, g)
                    for t in range(GROUP):
                        o = bank(4 + t // 4)[:, t % 4 * F:(t % 4 + 1) * F]
                        nc.tensor.matmul(o, NR[:, s, t, :], WO2G[:], start=True, stop=False)
                        m = nc.tensor.matmul(o, FE[:, s, t, :], WO2L[:], start=False, stop=True)
                    m.then_inc(projected, 1)

            @block.scalar
            def _(act):
                for g in range(NG):
                    s = g % 2
                    act.wait_ge(turned, g + 1)
                    wait(act, projected, g - 1)
                    act.copy(FT[:, s, 0:512], bank(0))
                    act.copy(FT[:, s, 512:GN], bank(1)[:, 0:GN - 512]).then_inc(turned_sb, 1)
                    act.wait_ge(hidden, g + 1)
                    for b, t, n in ((2, 0, 4), (3, 4, GROUP - 4)):
                        ps = bank(b)[:, 0:n * P].rearrange("p (t f) -> p t f", f=P)
                        act.activation(NR[:, s, t:t + n, :], ps, ACT.Gelu, bias=cols[:, 5:6], scale=SMU_S)
                        i = act.activation(FE[:, s, t:t + n, :], ps, ACT.Identity, bias=cols[:, 4:5])
                    i.then_inc(gelu_done, 1)
        clear()

        def post_edgeconv(onto_x):
            def post(dve, st, g, s):
                rows = NR[:, s, :, :]
                st.then(dve.tensor_tensor(rows, rows, BASE[:, gsl(g), :], ALU.add))
                if onto_x:
                    return dve.scalar_tensor_tensor(X[:, gsl(g), :], rows, 0.0, X[:, gsl(g), :],
                                                    ALU.max, ALU.add)
                return dve.tensor_single_scalar(FE[:, s, :, :], rows, 0.0, ALU.max)
            return post

        WE_flat = WE[:, :, :].rearrange("p l f -> p (l f)")
        bias_flat = bias_e[:, :, :].rearrange("p l f -> p (l f)")
        node_phase(None, 0, None, True, WE[:, 0, :], 2 * F, finish_edgeconv(bias_e[:, 0, :]))
        with nc.Fori(0, LAYERS - 1) as l:
            edge_pass(True, layer=l)
            node_phase(idx_max, l, post_edgeconv(False), False, WE_flat[:, ds((l + 1) * (2 * F), 2 * F)],
                       2 * F, finish_edgeconv(bias_flat[:, ds((l + 1) * F, F)]))
        passed(LAYERS - 1)
        rows_gathered(LAYERS - 1)
        edge_pass(True)
        passed()
        node_phase(idx_max, 0, post_edgeconv(True), True, W12[:, 0, :], F, finish_gcn)
        rows_gathered()

        edge_pass(False)
        passed()
        node_phase(idx_sum, 0, post_gcn(0), False, W12[:, 1, :], F, finish_gcn)
        rows_gathered()
        edge_pass(False)
        passed()
        base = list(total.rows)
        with nc.Block() as block:
            @block.gpsimd
            def _(pool):
                for g in range(NG):
                    s = g % 2
                    wait(pool, rows_used, g - 1)
                    for t in range(GROUP):
                        k = tile_cols(g, t)
                        pool.indirect_dma_start(NR[:, s, t, :], None, run_rows,
                                                bass.IndirectOffsetOnAxis(idx_sum[:, k:k + 1].bitcast(u32), 0))\
                            .then_inc(rows_landed[s], 16)

            @block.vector
            def _(dve):
                st = Steps(dve, order_v)
                for g in range(NG):
                    s = g % 2
                    rows = NR[:, s, :, :]
                    dve.wait_ge(rows_landed[s], base[s] + 16 * GROUP * (g // 2 + 1))
                    st.then(dve.tensor_tensor(rows, rows, TBL[:, gsl(g), :], ALU.add))
                    st.then(dve.tensor_tensor(rows, rows, per_node(g), ALU.mult))
                    st.then(dve.tensor_tensor(rows, rows, bias_g[:, 1, :].unsqueeze(1)
                                              .to_broadcast([P, GROUP, F]), ALU.add))
                    dve.tensor_tensor(X[:, gsl(g), :], X[:, gsl(g), :], rows, ALU.add).then_inc(rows_used, 1)

            @block.sync
            def _(sp):
                for g in range(NG):
                    sp.wait_ge(rows_used, g + 1)
                    whole = min(GROUP, N // P - g * GROUP)
                    sp.dma_start(out[g * GN:g * GN + whole * P, :].rearrange("(t p) f -> p t f", p=P),
                                 X[:, g * GROUP:g * GROUP + whole, :]).then_inc(table_out, 16)
                sp.dma_start(out[N // P * P:N, :], X[0:N % P, NT - 1, :]).then_inc(table_out, 16)
                sp.wait_ge(table_out, 16 * (NG + 1))


_INS = ["x", "src", "dst", "edge_attr_20", "edge_weight", "L0_gnn_W", "L0_gnn_b", "L0_gnn_gamma",
        "L0_gnn_beta", "L1_gnn_W_in2f", "L1_gnn_W_f1", "L1_gnn_b_f1", "L1_gnn_W_f2", "L1_gnn_b_f2",
        "L1_gnn_W_o1", "L1_gnn_b_o1", "L1_gnn_W_o2", "L1_gnn_b_o2", "L2_gnn_theta_w", "L2_gnn_theta_b",
        "L2_gnn_phi_w", "L2_gnn_phi_b", "L3_gnn_W1", "L3_gnn_b1", "L3_gnn_W2", "L3_gnn_b2"]


def kernel(**inputs):
    import numpy as np
    import concourse.bacc as bacc
    from concourse.bass_utils import run_bass_kernel_spmd

    nc = bacc.Bacc("TRN2", target_bir_lowering=False, num_devices=1)
    arrays, args = {}, []
    for name in _INS:
        a = np.ascontiguousarray(inputs[name])
        arrays[f"in_{name}"] = a
        args.append(nc.dram_tensor(f"in_{name}", a.shape, mybir.dt.from_np(a.dtype), kind="ExternalInput").ap())
    out = nc.dram_tensor("out", (N, F), mybir.dt.float32, kind="ExternalOutput").ap()
    gnn_kernel(nc, *args, out)
    return run_bass_kernel_spmd(nc, [arrays], core_ids=[0]).results[0]["out"]
```

```python
import concourse.bass as bass
from concourse import mybir
from contextlib import ExitStack

P = 128
N = 6250
E = 106250
F = 128
K_ATTR = 20
NT = -(-N // P)
N_PAD = NT * P
GROUP = 7
SIZES = [6] * 7 + [5, 2]
STARTS = [sum(SIZES[:g]) for g in range(len(SIZES))]
NG = len(SIZES)
GN = GROUP * P
UNROLL = 32
HALF = 16
T = -(-E // (P * UNROLL)) * UNROLL
ITERS = T // UNROLL
E_PAD = P * T
FULL = E // T
REST = E - FULL * T
RING = 8
QUAD = 4
CQ = HALF // QUAD
ACCS = 4
TB = -(-T // P)
BLOCK = 32
BLOCKS = T // BLOCK
BIG = 1.0e38
EPS = 1e-5
ALPHA = 0.01
SMU_S = 2.0 ** 0.5 * 2.5 * (1 - ALPHA)
SMU_G = (1 - ALPHA) / SMU_S
ROW_SUM = E_PAD
ROW_MAX = E_PAD + 1
LAYERS = 4
KA = QUAD * K_ATTR + 1
NW = 5 + 2 * LAYERS


assert sum(SIZES) == NT and max(SIZES) <= GROUP and T % BLOCK == 0 and E < E_PAD


def pieces(n, per):
    return [(t, min(per, n - t)) for t in range(0, n, per)]


def gnn_kernel(nc, x, src, dst, edge_attr, edge_weight, w0, b0, gamma, beta, w_in2f, w_f1, b_f1,
               w_f2, b_f2, w_o1, b_o1, w_o2, b_o2, theta_w, theta_b, phi_w, phi_b, w1, b1, w2, b2, out):
    f32, i32, u32, bf16 = mybir.dt.float32, mybir.dt.int32, mybir.dt.uint32, mybir.dt.bfloat16
    ALU = mybir.AluOpType
    ACT = mybir.ActivationFunctionType
    ds = bass.ds
    ctx = ExitStack()
    with ctx:
        def sb(name, shape, dt=f32):
            return ctx.enter_context(nc.sbuf_tensor(name, shape, dt))

        def dram(name, shape, dt=f32):
            return nc.dram_tensor(name, shape, dt, kind="Internal").ap()

        cleared = []

        def sem(name, phase=True):
            s = ctx.enter_context(nc.semaphore(name))
            if phase:
                cleared.append(s)
            return s

        def wait(eng, s, value):
            if not isinstance(value, int) or value > 0:
                eng.wait_ge(s, value)

        def hold(eng, s, value):
            if not isinstance(value, int) or value > 0:
                eng.wait_ge(s, value)
                if not isinstance(value, int):
                    eng.sem_inc(held[eng.engine], 1)

        table = dram("table", (N_PAD, F))
        run_rows = dram("run_rows", (E_PAD + 2, F))
        fill_rows = dram("fill_rows", (E_PAD + N_PAD, F))
        attr_pad = dram("attr_pad", (E_PAD, K_ATTR))
        src_rows = dram("src_rows", (2, T * P), bf16)
        dst_blocks = dram("dst_blocks", (P * BLOCKS + 1, BLOCK))
        acc_dram = [dram(f"acc{k}", (N_PAD + P, F)) for k in range(ACCS)]
        run_view = run_rows[0:E_PAD, :].rearrange("(p t) f -> p (t f)", t=T)
        fill_view = fill_rows[0:E_PAD, :].rearrange("(p t) f -> p (t f)", t=T)

        X = sb("X", [P, NT, F])
        TBL = sb("TBL", [P, NT, F])
        BASE = sb("BASE", [P, NT, F])
        HT = BASE[:, :, :].rearrange("p a b -> p (a b)")
        KEEP = sb("KEEP", [P, T])
        RESET = sb("RESET", [P, T])
        WEIGHT = sb("WEIGHT", [P, T])
        SRCF = sb("SRCF", [P, T])
        SCAT = sb("SCAT", [P, T])
        ident = sb("ident", [P, P])
        ones = sb("ones", [P, P])
        ones_bf = sb("ones_bf", [2, P], bf16)
        lower = sb("lower", [P, P])
        iota_p = sb("iota_p", [P, 1])
        iota_bf = sb("iota_bf", [P, P], bf16)
        iota_i = sb("iota_i", [P, P], i32)
        iota_pi = sb("iota_pi", [P, 1], i32)
        zeros = sb("zeros", [P, HALF * F])
        neutral = sb("neutral", [2, F])
        no_node = sb("no_node", [1, BLOCK])
        WORK = sb("WORK", [P, 4 * HALF * F])
        RUN = WORK[:, 0:2 * HALF * F].rearrange("p (h t f) -> p h t f", h=2, t=HALF)
        FILL = WORK[:, 2 * HALF * F:].rearrange("p (h t f) -> p h t f", h=2, t=HALF)
        ACC = WORK[:, 0:2 * ACCS * GROUP * F].rearrange("p (s k t f) -> p s k t f", s=2, k=ACCS, t=GROUP)

        def field(k, dt=f32):
            v = WORK[:, k * (T + 8):k * (T + 8) + T + 1]
            return v if dt == f32 else v.bitcast(dt)

        SRC, DP, LOI, HII = (field(k, i32) for k in range(4))
        SRC_LO, SRC_HI, DSTF = (field(k) for k in range(4, 7))
        LOB, HIB = field(7, bf16), field(8, bf16)
        deg = sb("deg", [P, NT])
        last_pad = sb("last_pad", [P, NT + 1])
        dinv = sb("dinv", [P, NT])
        tmpn = sb("tmpn", [P, 8, NT])
        idx_sum = sb("idx_sum", [P, NT], i32)
        idx_max = sb("idx_max", [P, NT], i32)
        idx_first = sb("idx_first", [P, NT], i32)
        seg = sb("seg", [P, 4])
        idx_patch = sb("idx_patch", [P, 1], i32)
        first_dst = sb("first_dst", [P, 1], i32)
        cont_cols = sb("cont_cols", [P, 2, P])
        CONT = sb("CONT", [P, P])
        CHAIN = sb("CHAIN", [P, P])
        CONT_R = sb("CONT_R", [P, P])
        CHAIN_R = sb("CHAIN_R", [P, P])
        upper = CONT_R
        stage = sb("stage", [P, 2, HALF], i32)
        G = sb("G", [P, RING, F])
        carry_t = sb("carry_t", [P, 2, P])
        patch = sb("patch", [P, 2, F])
        NR = sb("NR", [P, 2, GROUP, F])
        FE = sb("FE", [P, 2, GROUP, F])
        FT = sb("FT", [P, 2, GN])
        raw = NR[:, :, :, :].rearrange("p a b f -> p (a b) f")
        stats = sb("stats", [P, 2 * NG, 6])
        mv = sb("mv", [P, 2, GROUP, 2])
        norm = sb("norm", [P, 2, 3, GROUP])
        bnp = sb("bnp", [P, 8])
        WT = sb("WT", [P, 2, F])
        WO1 = sb("WO1", [P, F])
        WO2G = sb("WO2G", [P, F])
        WO2L = sb("WO2L", [P, F])
        WF2G = sb("WF2G", [P, F])
        WF2L = sb("WF2L", [P, F])
        WE = sb("WE", [P, LAYERS, 2 * F])
        W12 = sb("W12", [P, 2, F])
        cols = sb("cols", [P, 6])
        rowb = sb("rowb", [1, 4 + 2 * LAYERS, F])
        bias_o2 = sb("bias_o2", [P, F])
        bias_g = sb("bias_g", [P, 2, F])
        bias_e = sb("bias_e", [P, LAYERS, F])
        WB = sb("WB", [P, QUAD, KA])
        wf1 = sb("wf1", [P, K_ATTR])
        W1Q = sb("W1Q", [KA, QUAD, F])
        W21Q = sb("W21Q", [KA, QUAD, F])
        pick_one = sb("pick_one", [1, KA])
        AT = sb("AT", [P, 2, CQ, KA])
        ATT = sb("ATT", [KA, 4, P])
        GH = FT[:, :, 0:QUAD * P]
        HX = BASE[:, 0:2 * QUAD, :]
        MSG = BASE[:, 2 * QUAD:4 * QUAD, :].rearrange("p (s j) f -> p s j f", s=2)
        SAME = BASE[:, 4 * QUAD:8 * QUAD, :].rearrange("p (s j) f -> p s j f", s=4)
        TOT = sb("TOT", [P, 2, QUAD * F])
        SROW = sb("SROW", [2, 2, HALF * P], bf16)

        banks = [ctx.enter_context(nc.psum_tensor(f"bank{i}", [P, 1024], f32)) for i in range(4)]

        def gsl(g, first=0, n=None):
            a = STARTS[g] + first
            return slice(a, a + (SIZES[g] if n is None else n))

        def group_rows(ap, g):
            return ap[gsl(g).start * P:gsl(g).stop * P, :].rearrange("(t p) f -> p t f", p=P)

        def bank(i, n=1):
            return banks[i // 2][:, i % 2 * 512:(i % 2 + n) * 512]

        loads_s, loads_a, consts = sem("loads_s"), sem("loads_a"), sem("consts")
        order_v, order_p, order_a = sem("order_v"), sem("order_p"), sem("order_a")
        pe_done, cp_done = sem("pe_done"), sem("cp_done")
        blocks_ready, blocks_out = sem("blocks_ready"), sem("blocks_out")
        hot, counted = sem("hot"), sem("counted")
        ht_scaled, ht_turned = sem("ht_scaled"), sem("ht_turned")
        src_turned, src_sb = sem("src_turned"), sem("src_sb")
        staged, reduced = sem("staged"), sem("reduced")
        stored = [sem(f"stored{i}") for i in range(2)]
        zeroed = [sem(f"zeroed{i}") for i in range(2)]
        rows_in = [sem(f"rows_in{i}") for i in range(2)]
        fill_in = [sem(f"fill_in{i}") for i in range(2)]
        attr_in = [sem(f"attr_in{i}") for i in range(2)]
        acc_in = [sem(f"acc_in{i}") for i in range(2)]
        spread, compared = sem("spread"), sem("compared")
        attr_turned, attr_sb = sem("attr_turned"), sem("attr_sb")
        hidden, gelu_done, filtered = sem("hidden"), sem("gelu_done"), sem("filtered")
        expanded, messaged = sem("expanded"), sem("messaged")
        summed, totalled = sem("summed"), sem("totalled")
        held = {e.engine: sem(f"held_{n}") for n, e in (("sp", nc.sync), ("pool", nc.gpsimd))}
        based, bn_ready, bn_root, bn_done = sem("based"), sem("bn_ready"), sem("bn_root"), sem("bn_done")
        rows_used, var_ready, std_ready = sem("rows_used"), sem("var_ready"), sem("std_ready")
        norm_ready, feat_ready = sem("norm_ready"), sem("feat_ready")
        turned, turned_sb = sem("turned"), sem("turned_sb")
        projected, table_ready, evicted = sem("projected"), sem("table_ready"), sem("evicted")
        table_out = sem("table_out")
        agg_turned, agg_sb, agg_projected = sem("agg_turned"), sem("agg_sb"), sem("agg_projected")
        landed = [sem(f"landed{i}", phase=False) for i in range(RING)]
        rows_landed = [sem(f"rows_landed{i}", phase=False) for i in range(2)]
        patched = sem("patched", phase=False)
        firsts = sem("firsts", phase=False)
        x_in = sem("x_in", phase=False)
        added = [sem(f"added{k}", phase=False) for k in range(ACCS)]

        class Total:
            gathers = 0
            rows = [0, 0]
            patches = 0

        total = Total()

        def clear():
            with nc.Block() as block:
                @block.sync
                def _(sp):
                    for s in cleared[0::3]:
                        sp.sem_clear(s)

                @block.scalar
                def _(act):
                    for s in cleared[1::3]:
                        act.sem_clear(s)

                @block.tensor
                def _(pe):
                    for s in cleared[2::3]:
                        pe.sem_clear(s)

        class Steps:
            def __init__(self, eng, s):
                self.eng, self.s, self.n = eng, s, 0

            def did(self, ins):
                self.n += 1
                return ins.then_inc(self.s, 1)

            def join(self):
                wait(self.eng, self.s, self.n)

            def then(self, ins):
                self.did(ins)
                self.join()

        with nc.Block() as block:
            @block.gpsimd
            def _(pool):
                pool.memset(SRC[:, 0:T], 0).then_inc(consts, 1)
                pool.memset(DP[:, 1:T + 1], N).then_inc(consts, 1)
                pool.memset(DP[:, 0:1], -1).then_inc(consts, 1)
                pool.memset(WEIGHT[:], 0.0).then_inc(consts, 1)
                st = Steps(pool, order_p)
                st.did(pool.memset(ones[:], 1.0))
                st.did(pool.iota(iota_pi[:], [[1, 1]], base=0, channel_multiplier=1))
                st.did(pool.iota(iota_i[:], [[1, P]], base=0, channel_multiplier=0))
                st.join()
                pool.affine_select(out=ident[:], in_=ones[:], compare_op=ALU.is_equal, fill=0.0,
                                   base=0, pattern=[[-1, P]], channel_multiplier=1)
                pool.affine_select(out=lower[:], in_=ones[:], compare_op=ALU.is_ge, fill=0.0,
                                   base=0, pattern=[[-1, P]], channel_multiplier=1)
                pool.affine_select(out=upper[:], in_=ones[:], compare_op=ALU.is_ge, fill=0.0,
                                   base=0, pattern=[[1, P]], channel_multiplier=-1)

            @block.vector
            def _(dve):
                dve.memset(X[:, NT - 1, :], 0.0).then_inc(consts, 1)
                dve.memset(zeros[:], 0.0)
                dve.memset(neutral[:], -BIG)
                dve.memset(no_node[:], float(2 * N_PAD))
                dve.memset(ones_bf[:], 1.0)
                dve.memset(pick_one[:], 0.0)
                dve.memset(WB[:], 0.0)
                dve.memset(AT[:], 1.0)

            @block.sync
            def _(sp):
                n = 0

                def load(o, i, single=False):
                    nonlocal n
                    sp.dma_start(o, i, allow_slow_non_contiguous=single).then_inc(loads_s, 16)
                    n += 16

                sp.wait_ge(consts, 5)
                cut = FULL // 16 * 16
                for o, i in [(DP[:, 1:T + 1], dst), (SRC[:, 0:T], src), (WEIGHT[:, :], edge_weight)]:
                    load(o[0:cut, :], i[0:cut * T].rearrange("(p t) -> p t", t=T))
                    load(o[cut:FULL, :], i[cut * T:FULL * T].rearrange("(p t) -> p t", t=T))
                    load(o[FULL:FULL + 1, 0:REST], i[FULL * T:E].rearrange("(p t) -> p t", p=1))
                load(DP[1:FULL + 1, 0:1], dst[0:FULL * T].rearrange("(p t) -> p t", t=T)[:, T - 1:T], True)
                sp.dma_start(X[:, 0:NT - 1, :], x[0:(NT - 1) * P, :].rearrange("(t p) f -> p t f", p=P))\
                    .then_inc(x_in, 16)
                sp.dma_start(X[0:N - (NT - 1) * P, NT - 1, :], x[(NT - 1) * P:N, :]).then_inc(x_in, 16)
                sp.wait_ge(loads_s, n)

            @block.scalar
            def _(act):
                n = 0

                def load(o, i, single=False):
                    nonlocal n
                    act.dma_start(o, i, allow_slow_non_contiguous=single).then_inc(loads_a, 16)
                    n += 16

                for k, w in enumerate([w0, w_in2f, w_f2, w_o1, w_o2]):
                    load(raw[:, k, :], w)
                load(raw[:, 5:5 + LAYERS, :], theta_w.rearrange("l o i -> o l i"))
                load(raw[:, 5 + LAYERS:NW, :], phi_w.rearrange("l o i -> o l i"))
                load(wf1[:], w_f1)
                load(W12[:, 0, :], w1)
                load(W12[:, 1, :], w2)
                for k, b in enumerate([b0, gamma, beta, b_f1, b_o1]):
                    load(cols[:, k:k + 1], b.rearrange("(p a) -> p a", a=1))
                for k, b in enumerate([b_f2, b_o2, b1, b2]):
                    load(rowb[:, k, :], b.rearrange("(a n) -> a n", a=1))
                load(rowb[:, 4:4 + LAYERS, :], theta_b.rearrange("(a l) n -> a l n", a=1))
                load(rowb[:, 4 + LAYERS:, :], phi_b.rearrange("(a l) n -> a l n", a=1))
                act.wait_ge(loads_a, n)
        clear()

        with nc.Block() as block:
            @block.tensor
            def _(pe):
                for k in range(NW):
                    wait(pe, cp_done, k - 3)
                    nc.tensor.transpose(bank(k % 4)[:, 0:F], raw[:, k, :], ident[:]).then_inc(pe_done, 1)
                for k in range(3):
                    nc.tensor.matmul(bank(4)[:, k * F:(k + 1) * F], ones[0:1, :], rowb[:, 1 + k, :],
                                     start=True, stop=True)
                for l in range(LAYERS):
                    for k, first in ((4 + l, True), (4 + LAYERS + l, False)):
                        m = nc.tensor.matmul(bank(5)[:, l * F:(l + 1) * F], ones[0:1, :], rowb[:, k, :],
                                             start=first, stop=not first)
                m.then_inc(pe_done, 1)
                pe.wait_ge(order_p, 1)
                pe.wait_ge(cp_done, NW)
                for j in range(QUAD):
                    nc.tensor.transpose(bank(j)[0:KA, 0:F], WB[:, j, :], ident[:])
                    nc.tensor.matmul(bank(4 + j)[0:KA, 0:F] if j > 1 else bank(j)[0:KA, F:2 * F],
                                     WB[:, j, :], WF2L[:], start=True, stop=False)
                    m = nc.tensor.matmul(bank(4 + j)[0:KA, 0:F] if j > 1 else bank(j)[0:KA, F:2 * F],
                                         pick_one[:], rowb[:, 0, :], start=False, stop=True)
                m.then_inc(pe_done, 1)

            @block.scalar
            def _(act):
                for k in range(NW):
                    act.wait_ge(pe_done, k + 1)
                    p = bank(k % 4)[:, 0:F]
                    if k < 2:
                        last = act.copy(WT[:, k, :], p)
                    elif k in (2, 4):
                        g, lin = (WF2G, WF2L) if k == 2 else (WO2G, WO2L)
                        act.activation(g[:], p, ACT.Copy, scale=SMU_G)
                        last = act.activation(lin[:], p, ACT.Copy, scale=ALPHA)
                    elif k == 3:
                        last = act.copy(WO1[:], p)
                    else:
                        which, l = divmod(k - 5, LAYERS)
                        last = act.copy(WE[:, l, 0:F] if which == 0 else BASE[:, l, :], p)
                    last.then_inc(cp_done, 1)
                act.wait_ge(pe_done, NW + 1)
                act.copy(bias_o2[:], bank(4)[:, 0:F])
                act.copy(bias_g[:, :, :].rearrange("p a b -> p (a b)"), bank(4)[:, F:3 * F])
                act.copy(bias_e[:, :, :].rearrange("p a b -> p (a b)"), bank(5))
                act.wait_ge(pe_done, NW + 2)
                for j in range(QUAD):
                    act.copy(W1Q[:, j, :], bank(j)[0:KA, 0:F])
                    act.copy(W21Q[:, j, :], bank(4 + j)[0:KA, 0:F] if j > 1 else bank(j)[0:KA, F:2 * F])
                act.activation(cols[:, 5:6], cols[:, 4:5], ACT.Copy, scale=SMU_S)

            @block.gpsimd
            def _(pool):
                for j in range(QUAD):
                    pool.tensor_copy(WB[:, j, j * K_ATTR:(j + 1) * K_ATTR], wf1[:])
                    pool.tensor_copy(WB[:, j, KA - 1:KA], cols[:, 3:4])
                pool.memset(pick_one[:, KA - 1:KA], 1.0).then_inc(order_p, 1)
                pool.tensor_copy(first_dst[:], DP[:, 1:2])
                pool.affine_select(out=G[:, 0, :], in_=ones[:], compare_op=ALU.is_equal, fill=0.0,
                                   base=1, pattern=[[-1, P]], channel_multiplier=1)
                pool.affine_select(out=G[:, 1, :], in_=ones[:], compare_op=ALU.is_ge, fill=0.0,
                                   base=1 - P, pattern=[[-1, P]], channel_multiplier=1)

            @block.vector
            def _(dve):
                st = Steps(dve, order_v)
                st.did(dve.tensor_tensor(KEEP[:], DP[:, 0:T], DP[:, 1:T + 1], ALU.is_equal))
                st.did(dve.tensor_copy(iota_p[:], iota_pi[:]))
                st.did(dve.tensor_copy(iota_bf[:], iota_i[:]))
                st.did(dve.tensor_copy(SRCF[:], SRC[:, 0:T]))
                st.did(dve.tensor_copy(DSTF[:, 0:T], DP[:, 1:T + 1]))
                st.did(dve.tensor_single_scalar(LOI[:, 0:T], DP[:, 1:T + 1], P - 1, ALU.bitwise_and))
                st.did(dve.tensor_single_scalar(HII[:, 0:T], DP[:, 1:T + 1], 7, ALU.logical_shift_right))
                st.join()
                st.did(dve.tensor_copy(LOB[:, 0:T], LOI[:, 0:T]))
                st.did(dve.tensor_copy(HIB[:, 0:T], HII[:, 0:T]))
                st.did(dve.tensor_scalar(RESET[:], KEEP[:], -1.0, BIG, ALU.add, ALU.mult))
                st.did(dve.tensor_copy(seg[:, 3:4], DSTF[:, 0:1]))
                st.did(dve.tensor_copy(seg[:, 2:3], KEEP[:, 0:1]))
                st.join()
                st.did(dve.tensor_scalar(SCAT[:], DSTF[:, 0:T], seg[:, 3:4], 0.0, ALU.is_equal, ALU.add,
                                         accum_out=seg[:, 0:1]))
                st.did(dve.tensor_single_scalar(LOI[:, 0:T], SRC[:, 0:T], P - 1, ALU.bitwise_and))
                st.join()
                st.did(dve.tensor_single_scalar(seg[:, 1:2], seg[:, 0:1], float(T), ALU.is_equal))
                st.did(dve.tensor_scalar(seg[:, 3:4], iota_p[:], float(T), -1.0, ALU.mult, ALU.add))
                st.did(dve.tensor_copy(SRC_LO[:, 0:T], LOI[:, 0:T]))
                st.join()
                st.did(dve.tensor_tensor(SRC_HI[:, 0:T], SRCF[:], SRC_LO[:, 0:T], ALU.subtract))
                st.did(dve.tensor_tensor(seg[:, 3:4], seg[:, 3:4], seg[:, 0:1], ALU.add))
                st.did(dve.tensor_copy(cont_cols[:, 0, :], seg[:, 2:3].to_broadcast([P, P])))
                st.did(dve.tensor_copy(cont_cols[:, 1, :], seg[:, 1:2].to_broadcast([P, P])))
                st.join()
                dve.tensor_copy(idx_patch[:], seg[:, 3:4])
                dve.wait_ge(cp_done, NW)
                dve.tensor_tensor(WE[:, :, F:2 * F], BASE[:, 0:LAYERS, :], WE[:, :, 0:F], ALU.subtract)
        clear()

        OL = WORK[:, 0:BLOCKS * P // 2].bitcast(bf16)
        ohl = OL.rearrange("p (t n) -> p t n", t=BLOCKS)
        OH = WORK[:, BLOCKS * P // 2:BLOCKS * (P + NT + 1) // 2].bitcast(bf16)
        ohh = OH.rearrange("p (t n) -> p t n", t=BLOCKS)[:, :, 0:NT]
        first_free = BLOCKS * (P + NT + 1) // 2
        SRC_T = WORK[:, first_free:first_free + TB * P].bitcast(bf16)
        assert first_free + TB * P <= 4 * (T + 8)
        srct = SRC_T[:, 0:2 * TB * P].rearrange("t (k b p) -> t k b p", k=2, b=TB)
        BLK = NR[:, :, :, :].rearrange("p a b f -> p (a b f)")[:, 0:NT * BLOCK]\
            .rearrange("p (t e) -> p t e", e=BLOCK)
        splits = [range(0, NT // 2), range(NT // 2, NT)]
        halves = [[(a, min(a + SIZES[g] * P // 2, N)) for a in
                   (STARTS[g] * P, STARTS[g] * P + SIZES[g] * P // 2)] for g in range(NG)]

        def table_row(ap, column):
            return bass.IndirectOffsetOnAxis(column.bitcast(u32), 0)

        def node_stats(dve, st, g):
            s, n = g % 2, SIZES[g]
            for t in range(n):
                st.did(dve.bn_stats(stats[:, t, :], X[:, STARTS[g] + t, :]))
            st.join()
            wait(dve, feat_ready, g - 1)
            for t in range(n):
                st.did(dve.bn_aggr(mv[:, s, t, :], stats[:, t, :]))
            st.join()
            dve.tensor_single_scalar(norm[:, s, 0, 0:n], mv[:, s, 0:n, 1], EPS, ALU.add).then_inc(var_ready, 1)

        def node_scale(dve, st, g):
            s, n = g % 2, SIZES[g]
            dve.wait_ge(std_ready, g + 1)
            st.then(dve.reciprocal(norm[:, s, 1, 0:n], norm[:, s, 0, 0:n]))
            dve.scalar_tensor_tensor(norm[:, s, 2, 0:n], mv[:, s, 0:n, 0], -1.0, norm[:, s, 1, 0:n],
                                     ALU.mult, ALU.mult).then_inc(norm_ready, 1)

        def node_norm(act, g):
            s, n = g % 2, SIZES[g]
            act.wait_ge(var_ready, g + 1)
            act.activation(norm[:, s, 0, 0:n], norm[:, s, 0, 0:n], ACT.Sqrt).then_inc(std_ready, 1)
            act.wait_ge(norm_ready, g + 1)
            wait(act, turned, g - 1)
            for t in range(n):
                i = act.activation(FE[:, s, t, :], X[:, STARTS[g] + t, :], ACT.Relu,
                                   bias=norm[:, s, 2, t:t + 1], scale=norm[:, s, 1, t:t + 1])
            i.then_inc(feat_ready, 1)

        def turn_features(pe, g, b, source=None):
            for t in range(SIZES[g]):
                m = nc.tensor.transpose(bank(b + t // 4)[:, t % 4 * P:(t % 4 + 1) * P],
                                        FE[:, g % 2, t, :] if source is None else source(t), ident[:])
            return m

        def copy_turned(act, g, b):
            act.wait_ge(turned, g + 1)
            wait(act, projected, g - 1)
            for t, n in pieces(SIZES[g], 4):
                i = act.copy(FT[:, g % 2, t * P:(t + n) * P], bank(b + t // 4)[:, 0:n * P])
            i.then_inc(turned_sb, 1)

        def store_table(sp):
            for g in range(NG):
                sp.wait_ge(table_ready, g + 1)
                sp.dma_start(group_rows(table, g), TBL[:, gsl(g), :]).then_inc(table_out, 16)

        with nc.Block() as block:
            @block.vector
            def _(dve):
                st = Steps(dve, order_v)
                le, tile, upto, last, first, has, root, node = (tmpn[:, k, :] for k in range(8))
                dve.tensor_tensor(ohl, iota_bf[:, :].unsqueeze(1).to_broadcast([P, BLOCKS, P]),
                                  LOB[:, BLOCK - 1:T:BLOCK].unsqueeze(2).to_broadcast([P, BLOCKS, P]),
                                  ALU.is_equal).then_inc(hot, 1)
                dve.tensor_tensor(ohh, iota_bf[:, 0:NT].unsqueeze(1).to_broadcast([P, BLOCKS, NT]),
                                  HIB[:, BLOCK - 1:T:BLOCK].unsqueeze(2).to_broadcast([P, BLOCKS, NT]),
                                  ALU.is_equal).then_inc(hot, 1)
                st.did(dve.tensor_copy(node, iota_i[:, 0:NT]))
                st.join()
                st.then(dve.tensor_scalar(node, node, float(P), iota_p[:, 0:1], ALU.mult, ALU.add))
                dve.wait_ge(counted, 1)
                dve.tensor_copy(deg[:], bank(0)[:, 0:NT]).then_inc(cp_done, 1)
                dve.wait_ge(x_in, 32)
                node_stats(dve, st, 0)
                node_scale(dve, st, 0)
                dve.wait_ge(pe_done, 1)
                st.did(dve.tensor_copy(le, bank(7)[:, 0:NT]))
                st.did(dve.tensor_copy(tile, bank(7)[:, 64:64 + NT]))
                st.did(dve.tensor_copy(CONT[:], bank(6)[:, 0:P]))
                st.did(dve.tensor_copy(CHAIN_R[:], bank(6)[:, P:2 * P]))
                st.did(dve.memset(CHAIN[:], 0.0))
                st.join()
                st.then(dve.tensor_tensor_scan(upto, ones[:, 0:NT], tile, 0.0, ALU.mult, ALU.add))
                st.then(dve.tensor_tensor(upto, upto, tile, ALU.subtract))
                st.then(dve.tensor_tensor(upto, upto, le, ALU.add))
                dve.tensor_copy(idx_first[:], upto).then_inc(blocks_ready, 1)
                for g in range(1, NG):
                    node_stats(dve, st, g)
                    node_scale(dve, st, g)
                k = 0
                for g in range(NG):
                    dve.wait_ge(evicted, g + 1)
                    for a, b in halves[g]:
                        st.did(dve.bn_stats(stats[:, k, :], HT[:, a:b]))
                        k += 1
                st.join()
                st.then(dve.bn_aggr(bnp[:, 0:2], stats[:, :, :].rearrange("p a b -> p (a b)")))
                dve.tensor_single_scalar(bnp[:, 2:3], bnp[:, 1:2], EPS, ALU.add).then_inc(bn_ready, 1)
                dve.wait_ge(bn_root, 1)
                st.then(dve.reciprocal(bnp[:, 3:4], bnp[:, 2:3]))
                st.then(dve.tensor_tensor(bnp[:, 4:5], bnp[:, 3:4], cols[:, 1:2], ALU.mult))
                st.then(dve.tensor_tensor(bnp[:, 5:6], bnp[:, 0:1], bnp[:, 4:5], ALU.mult))
                dve.tensor_tensor(bnp[:, 6:7], cols[:, 2:3], bnp[:, 5:6], ALU.subtract).then_inc(bn_done, 1)
                for k, tiles in enumerate(splits):
                    dve.wait_ge(rows_landed[k], 16 * len(tiles))
                    for t in tiles:
                        st.did(dve.tensor_scalar(BLK[:, t, :], BLK[:, t, :], node[:, t:t + 1], 0.0,
                                                 ALU.is_le, ALU.add, accum_out=le[:, t:t + 1]))
                st.then(dve.memset(last_pad[:, 0:1], 0.0))
                dve.scalar_tensor_tensor(last_pad[:, 1:NT + 1], upto, float(BLOCK), le, ALU.mult, ALU.add)\
                    .then_inc(cp_done, 1)
                dve.wait_ge(pe_done, 2)
                st.then(dve.tensor_copy(first, bank(7)[:, 0:NT]))
                dve.tensor_tensor(deg[:], last_pad[:, 1:NT + 1], first, ALU.subtract).then_inc(cp_done, 1)
                dve.wait_ge(cp_done, 3)
                dve.tensor_single_scalar(has, deg[:], 1.0, ALU.min).then_inc(order_v, 1)
                st.n += 1
                dve.wait_ge(order_a, 1)
                st.did(dve.reciprocal(dinv[:], root))
                st.join()
                for g in range(NG):
                    dve.wait_ge(ht_turned, g + 1)
                    for t, n in pieces(SIZES[g], 4):
                        i = dve.tensor_tensor(TBL[:, gsl(g, t, n), :],
                                              bank(2 + 2 * (g % 2) + t // 4)[:, 0:n * P]
                                              .rearrange("p (t f) -> p t f", f=F),
                                              dinv[:, gsl(g, t, n)].unsqueeze(2).to_broadcast([P, n, F]), ALU.mult)
                    i.then_inc(table_ready, 1)
                st.then(dve.tensor_single_scalar(last, last_pad[:, 1:NT + 1], -1.0, ALU.add))
                for o, row in ((idx_sum, ROW_SUM), (idx_max, ROW_MAX)):
                    st.then(dve.tensor_single_scalar(le, last, -float(row), ALU.add))
                    st.then(dve.tensor_tensor(le, le, has, ALU.mult))
                    st.then(dve.tensor_single_scalar(le, le, float(row), ALU.add))
                    st.then(dve.tensor_copy(o[:], le))
                st.then(dve.tensor_single_scalar(node, node, float(E_PAD), ALU.add))
                st.then(dve.tensor_tensor(le, first, node, ALU.subtract))
                st.then(dve.tensor_tensor(le, le, has, ALU.mult))
                st.then(dve.tensor_tensor(le, le, node, ALU.add))
                st.did(dve.tensor_copy(idx_first[:], le))
                st.did(dve.tensor_tensor(CHAIN[:, 1:P], CONT[:, 1:P], CHAIN_R[:, 0:P - 1], ALU.mult))
                st.did(dve.tensor_scalar(CONT_R[:], CONT[:], -1.0, BIG, ALU.add, ALU.mult))
                st.join()
                st.did(dve.tensor_scalar(CHAIN_R[:], CHAIN[:], -1.0, BIG, ALU.add, ALU.mult))

            @block.tensor
            def _(pe):
                def first_product(g):
                    pe.wait_ge(feat_ready, g + 1)
                    wait(pe, turned_sb, g)
                    turn_features(pe, g, 2).then_inc(turned, 1)
                    pe.wait_ge(turned_sb, g + 1)
                    wait(pe, evicted, g)
                    for t, n in pieces(SIZES[g], 4):
                        m = nc.tensor.matmul(bank(4 + t // 4)[:, 0:n * P], WT[:, 0, :],
                                             FT[:, g % 2, t * P:(t + n) * P], start=True, stop=True)
                    m.then_inc(projected, 1)

                pe.wait_ge(hot, 2)
                for t in range(BLOCKS):
                    m = nc.tensor.matmul(bank(0)[:, 0:NT], ohl[:, t, :], ohh[:, t, :],
                                         start=t == 0, stop=t == BLOCKS - 1)
                m.then_inc(counted, 1)
                pe.wait_ge(cp_done, 1)
                nc.tensor.matmul(bank(7)[:, 0:NT], upper[:], deg[:], start=True, stop=True)
                nc.tensor.matmul(bank(7)[:, 64:64 + NT], ones[:], deg[:], start=True, stop=True)
                nc.tensor.matmul(bank(6)[:, 0:P], cont_cols[:, 0, :], ident[:], start=True, stop=True)
                nc.tensor.matmul(bank(6)[:, P:2 * P], cont_cols[:, 1, :], ident[:], start=True,
                                 stop=True).then_inc(pe_done, 1)
                first_product(0)
                for k in range(2 * TB):
                    which, b = divmod(k, TB)
                    w = min(P, T - b * P)
                    wait(pe, src_sb, k)
                    nc.tensor.transpose(bank(1)[0:w, 0:P], (SRC_HI, SRC_LO)[which][:, b * P:b * P + w],
                                        ident[:]).then_inc(src_turned, 1)
                for g in range(1, NG):
                    first_product(g)
                pe.wait_ge(cp_done, 2)
                nc.tensor.matmul(bank(7)[:, 0:NT], G[:, 0, :], last_pad[:, 1:NT + 1], start=True, stop=False)
                nc.tensor.matmul(bank(7)[:, 0:NT], G[:, 1, :], last_pad[:, 0:NT], start=False,
                                 stop=True).then_inc(pe_done, 1)
                for g in range(NG):
                    pe.wait_ge(ht_scaled, g + 1)
                    wait(pe, table_ready, g - 1)
                    turn_features(pe, g, 2 + 2 * (g % 2),
                                  lambda t: HT[:, (STARTS[g] + t) * P:(STARTS[g] + t + 1) * P])\
                        .then_inc(ht_turned, 1)

            @block.scalar
            def _(act):
                def first_rows(g):
                    act.wait_ge(projected, g + 1)
                    for t, n in pieces(SIZES[g], 4):
                        i = act.activation(HT[:, (STARTS[g] + t) * P:(STARTS[g] + t + n) * P],
                                           bank(4 + t // 4)[:, 0:n * P], ACT.Identity, bias=cols[:, 0:1])
                    i.then_inc(evicted, 1)

                for g in range(NG):
                    node_norm(act, g)
                    if g > 0:
                        first_rows(g - 1)
                    copy_turned(act, g, 2)
                    if g > 0:
                        continue
                    for k in range(2 * TB):
                        which, b = divmod(k, TB)
                        w = min(P, T - b * P)
                        act.wait_ge(src_turned, k + 1)
                        act.copy(srct[0:w, which, b, :], bank(1)[0:w, 0:P]).then_inc(src_sb, 1)
                first_rows(NG - 1)
                act.wait_ge(bn_ready, 1)
                act.activation(bnp[:, 2:3], bnp[:, 2:3], ACT.Sqrt).then_inc(bn_root, 1)
                act.wait_ge(bn_done, 1)
                for g in range(NG):
                    h = HT[:, STARTS[g] * P:(STARTS[g] + SIZES[g]) * P]
                    act.activation(h, h, ACT.Identity, bias=bnp[:, 6:7], scale=bnp[:, 4:5])\
                        .then_inc(ht_scaled, 1)
                act.wait_ge(cp_done, 3)
                act.activation(tmpn[:, 6, :], deg[:], ACT.Sqrt, bias=ones[:, 0:1]).then_inc(order_a, 1)

            @block.gpsimd
            def _(pool):
                pool.wait_ge(blocks_ready, 1)
                pool.wait_ge(blocks_out, 32)
                for k, tiles in enumerate(splits):
                    for t in tiles:
                        pool.indirect_dma_start(BLK[:, t, :], None, dst_blocks,
                                                table_row(dst_blocks, idx_first[:, t:t + 1]))\
                            .then_inc(rows_landed[k], 16)
                    total.rows[k] += 16 * len(tiles)

            @block.sync
            def _(sp):
                n = 0

                def store(o, i):
                    nonlocal n
                    sp.dma_start(o, i).then_inc(loads_s, 16)
                    n += 16
                sp.dma_start(dst_blocks[0:P * BLOCKS, :].rearrange("(p t) e -> p (t e)", p=P),
                             DSTF[:, 0:T]).then_inc(blocks_out, 16)
                sp.dma_start(dst_blocks[P * BLOCKS:, :], no_node[:]).then_inc(blocks_out, 16)
                store(run_rows[ROW_SUM:ROW_SUM + 1, :], zeros[0:1, 0:F])
                store(run_rows[ROW_MAX:ROW_MAX + 1, :], neutral[0:1, :])
                store(attr_pad.rearrange("e k -> (e k)")[0:E * K_ATTR].rearrange("(a b) -> a b", a=50),
                      edge_attr.rearrange("e k -> (e k)").rearrange("(a b) -> a b", a=50))
                store(attr_pad[E:E + P, :], zeros[:, 0:K_ATTR])
                left = E_PAD - E - P
                if left > 0:
                    store(attr_pad[E + P:E_PAD, :], zeros[0:left, 0:K_ATTR])
                for k in range(ACCS):
                    rows = acc_dram[k].rearrange("(p t) f -> p (t f)", p=P)
                    for a, w in pieces((NT + 1) * F, HALF * F):
                        store(rows[:, a:a + w], zeros[:, 0:w])
                sp.wait_ge(src_sb, 2 * TB)
                for k in range(2):
                    rows = src_rows[k, :].rearrange("(t p) -> t p", p=P)
                    full = T // P
                    store(rows[0:full * P, :].rearrange("(b t) p -> t b p", t=P), srct[:, k, 0:full, :])
                    store(rows[full * P:T, :], srct[0:T - full * P, k, full, :])
                store_table(sp)
                sp.wait_ge(loads_s, n)
                sp.wait_ge(table_out, 16 * NG)
        clear()

        def update(block, index, base, post, norm_x, weights, finish, before=None, scatter=False):
            before = before or {}
            on_v, on_a = finish
            lag = 2 if norm_x else 1

            def firsts_out(pool, g):
                if g == 0:
                    for h in range(2):
                        pool.wait_ge(zeroed[h], 16 * ITERS)
                pool.wait_ge(table_ready, g + 1)
                for t in range(SIZES[g]):
                    k = STARTS[g] + t
                    pool.indirect_dma_start(fill_rows, table_row(fill_rows, idx_first[:, k:k + 1]),
                                            TBL[:, k, :], None).then_inc(firsts, 16)

            @block.gpsimd
            def _(pool):
                if "pool" in before:
                    before["pool"](pool)
                if index is not None:
                    for g in range(NG):
                        s = g % 2
                        wait(pool, rows_used, g - 1)
                        for t in range(SIZES[g]):
                            k = STARTS[g] + t
                            pool.indirect_dma_start(NR[:, s, t, :], None, run_rows,
                                                    table_row(run_rows, index[:, k:k + 1]))\
                                .then_inc(rows_landed[s], 16)
                        if scatter and g > lag:
                            firsts_out(pool, g - lag - 1)
                if scatter:
                    for g in range(NG - lag - 1, NG):
                        firsts_out(pool, g)
                    pool.wait_ge(firsts, 16 * NT)

            @block.vector
            def _(dve):
                st = Steps(dve, order_v)
                if "dve" in before:
                    before["dve"](dve, st)

                def front(g):
                    s = g % 2
                    if index is not None:
                        dve.wait_ge(rows_landed[s], base[s] + 16 * sum(SIZES[s:g + 1:2]))
                        if not norm_x:
                            wait(dve, turned, g - 1)
                        post(dve, st, g, s).then_inc(rows_used, 1)
                        dve.wait_ge(rows_used, g + 1)
                    if norm_x:
                        node_stats(dve, st, g)
                        node_scale(dve, st, g)

                for g in range(NG + lag):
                    if g < NG:
                        front(g)
                    if g >= lag and on_v is not None:
                        dve.wait_ge(projected, g - lag + 1)
                        on_v(dve, g - lag)

            @block.scalar
            def _(act):
                if "act" in before:
                    before["act"](act)

                def rows(g):
                    if on_a is not None:
                        act.wait_ge(projected, g + 1)
                        on_a(act, g)

                if norm_x:
                    for g in range(NG + 2):
                        if 1 <= g <= NG:
                            copy_turned(act, g - 1, 0)
                        if g < NG:
                            node_norm(act, g)
                        if g >= 2:
                            rows(g - 2)
                else:
                    for g in range(NG):
                        copy_turned(act, g, 0)
                        rows(g)

            @block.tensor
            def _(pe):
                if "pe" in before:
                    before["pe"](pe)
                for g in range(NG):
                    pe.wait_ge(feat_ready if norm_x else rows_used, g + 1)
                    wait(pe, turned_sb, g)
                    turn_features(pe, g, 0).then_inc(turned, 1)
                    pe.wait_ge(turned_sb, g + 1)
                    wait(pe, table_ready, g - 1 if len(weights) == 1 else g)
                    if on_v is not None and on_a is not None:
                        wait(pe, based, g)
                    for k, weight in enumerate(weights):
                        for t in range(SIZES[g]):
                            first = 2 + 2 * (k if len(weights) > 1 else g % 2)
                            m = nc.tensor.matmul(bank(first + t // 4)[:, t % 4 * F:(t % 4 + 1) * F],
                                                 FT[:, g % 2, t * P:(t + 1) * P], weight,
                                                 start=True, stop=True)
                    m.then_inc(projected, 1)

            @block.sync
            def _(sp):
                if "sp" in before:
                    before["sp"](sp)
                store_table(sp)
                sp.wait_ge(table_out, 16 * NG)

        def passing(maximum, times, pbase, leaders=False):
            base = total.gathers + times * (16 * T // RING)
            scale = RESET if maximum else KEEP
            op0, op1 = (ALU.add, ALU.max) if maximum else (ALU.mult, ALU.add)
            neutral_value = -BIG if maximum else 0.0
            tail = ((0, 8), (8, 6), (14, 2))
            stored_all = (16 * ITERS, 16 * (ITERS - 1 + len(tail)))

            def pool_part(pool):
                def body(it):
                    for j in range(UNROLL):
                        h, s = j // HALF, j % RING
                        if j % HALF == 0:
                            hold(pool, staged, it * 2 + h + 1)
                        if j % 2 == 0:
                            hold(pool, reduced, it * UNROLL + j - RING + 2)
                        pool.indirect_dma_start(G[:, s, :], None, table,
                                                table_row(table, stage[:, h, j % HALF:j % HALF + 1]))\
                            .then_inc(landed[s], 16)
                body(0)
                with pool.Fori(1, ITERS) as it:
                    body(it)
                for h in range(2):
                    pool.wait_ge(stored[h], stored_all[h])
                pool.indirect_dma_start(patch[:, 0, :], None, run_rows, table_row(run_rows, idx_patch[:]))\
                    .then_inc(patched, 16)
                pool.wait_ge(cp_done, 2)
                pool.indirect_dma_start(run_rows, table_row(run_rows, idx_patch[:]), patch[:, 1, :], None)\
                    .then_inc(patched, 16)
                hold(pool, patched, pbase + 32)

            def act_part(act):
                def body(it):
                    for h in range(2):
                        wait(act, reduced, (it * 2 + h - 1) * HALF)
                        act.copy(stage[:, h, :], SRCF[:, ds(it * UNROLL + h * HALF, HALF)]).then_inc(staged, 1)
                body(0)
                with act.Fori(1, ITERS) as it:
                    body(it)

            def dve_part(dve, st):
                st.then(dve.memset(RUN[:, 1, HALF - 1, :], neutral_value))

                def body(it):
                    for j in range(UNROLL):
                        h, k, s = j // HALF, j % HALF, j % RING
                        t = it * UNROLL + j
                        if k == 0:
                            wait(dve, stored[h], it * 16)
                        dve.wait_ge(landed[s], base + it * (16 * UNROLL // RING) + 16 * (j // RING + 1))
                        wait(dve, reduced, t)
                        hp, kp = (h, k - 1) if k else (1 - h, HALF - 1)
                        dve.scalar_tensor_tensor(RUN[:, h, k, :], RUN[:, hp, kp, :], scale[:, ds(t, 1)],
                                                 G[:, s, :], op0, op1).then_inc(reduced, 1)
                        if leaders:
                            q = j // QUAD
                            if j % QUAD == 0:
                                dve.wait_ge(spread, it * (UNROLL // QUAD) + q + 1)
                                wait(dve, compared, t - QUAD)
                            dve.scalar_tensor_tensor(FT[:, 0, j % (2 * QUAD) * P:(j % (2 * QUAD) + 1) * P]
                                                     if j % (2 * QUAD) < GROUP else NR[:, 0, 0, :],
                                                     bank(q % 2)[:, j % QUAD * P:(j % QUAD + 1) * P],
                                                     SRCF[:, ds(t, 1)], lower[:], ALU.is_equal, ALU.mult,
                                                     accum_out=SCAT[:, ds(t, 1)]).then_inc(compared, 1)
                body(0)
                with dve.Fori(1, ITERS) as it:
                    body(it)
                st.then(dve.memset(carry_t[:, 0, :], neutral_value))
                dve.wait_ge(pe_done, 1)
                st.then(dve.tensor_tensor(carry_t[:, 0, 1:P], bank(0)[:, 0:P - 1],
                                          (CONT_R if maximum else CONT)[:, 1:P],
                                          ALU.add if maximum else ALU.mult))
                dve.tensor_tensor_scan(carry_t[:, 1, :], (CHAIN_R if maximum else CHAIN)[:],
                                       carry_t[:, 0, :], neutral_value, op0, op1).then_inc(cp_done, 1)
                dve.wait_ge(pe_done, 2)
                dve.wait_ge(patched, pbase + 16)
                dve.tensor_tensor(patch[:, 1, :], patch[:, 0, :], bank(1)[:, 0:P], op1).then_inc(cp_done, 1)
                if leaders:
                    trash = FILL[:, 0, 0:7, :].rearrange("p a b -> p (a b)")[:, 0:T]
                    st.then(dve.tensor_single_scalar(seg[:, 3:4], iota_p[:], float(N_PAD), ALU.add))
                    st.did(dve.tensor_single_scalar(SCAT[:], SCAT[:], 1.0, ALU.is_equal))
                    st.did(dve.tensor_scalar(trash, SRCF[:], seg[:, 3:4], None, ALU.subtract))
                    st.join()
                    st.then(dve.tensor_tensor(SCAT[:], SCAT[:], trash, ALU.mult))
                    st.then(dve.tensor_scalar(SCAT[:], SCAT[:], seg[:, 3:4], None, ALU.add))

            def pe_part(pe):
                def body(it):
                    for q in range(UNROLL // QUAD):
                        h, k = q // CQ, q % CQ
                        if k == 0:
                            pe.wait_ge(rows_in[h], it * 16 + 16)
                        wait(pe, compared, it * UNROLL + (q - 1) * QUAD)
                        nc.tensor.matmul(bank(q % 2), ones_bf[:], SROW[:, h, k * QUAD * P:(k + 1) * QUAD * P],
                                         start=True, stop=True).then_inc(spread, 1)
                if leaders:
                    body(0)
                    with pe.Fori(1, ITERS) as it:
                        body(it)
                    pe.wait_ge(compared, T)
                pe.wait_ge(reduced, T)
                nc.tensor.transpose(bank(0)[:, 0:P], RUN[:, 1, HALF - 1, :], ident[:]).then_inc(pe_done, 1)
                pe.wait_ge(cp_done, 1)
                nc.tensor.transpose(bank(1)[:, 0:P], carry_t[:, 1, :], ident[:]).then_inc(pe_done, 1)
                pe.wait_ge(cp_done, 2)

            def sp_part(sp):
                def load_src(c, h):
                    hold(sp, spread, (c - 1) * CQ)
                    sp.dma_start(SROW[:, h, :], src_rows[:, ds(c * HALF * P, HALF * P)]).then_inc(rows_in[h], 16)

                def store(c, h, first, n):
                    hold(sp, reduced, c * HALF + first + n)
                    sp.dma_start(run_view[:, ds((c * HALF + first) * F, n * F)],
                                 RUN[:, h, first:first + n, :].rearrange("p t f -> p (t f)")).then_inc(stored[h], 16)

                def body(it, last=False):
                    for h in range(2):
                        c = it * 2 + h
                        if leaders:
                            if not (last and h == 1):
                                load_src(c + 1, 1 - h)
                            hold(sp, zeroed[h], it * 16)
                            hold(sp, reduced, c * HALF + HALF // 2)
                            sp.dma_start(fill_view[:, ds(c * HALF * F, HALF * F)], zeros[:])\
                                .then_inc(zeroed[h], 16)
                        if last and h == 1:
                            for first, n in tail:
                                store(c, h, first, n)
                        else:
                            store(c, h, 0, HALF)
                if leaders:
                    load_src(0, 0)
                body(0)
                with sp.Fori(1, ITERS - 1) as it:
                    body(it)
                body(ITERS - 1, last=True)
                for h in range(2):
                    sp.wait_ge(stored[h], stored_all[h])
                    if leaders:
                        sp.wait_ge(zeroed[h], 16 * ITERS)

            return {"pool": pool_part, "act": act_part, "dve": dve_part, "pe": pe_part, "sp": sp_part}

        def layer(maximum, index, post, norm_x, weights, finish, times=0, runs=1, leaders=False,
                  scatter=False):
            before = passing(maximum, times, total.patches + times * 32, leaders)
            base = [total.rows[s] + times * 16 * sum(SIZES[s::2]) for s in range(2)]
            with nc.Block() as block:
                update(block, index, base, post, norm_x, weights, finish, before, scatter)
            clear()
            total.gathers += runs * (16 * T // RING)
            total.patches += runs * 32
            for s in range(2):
                total.rows[s] += runs * 16 * sum(SIZES[s::2])

        def post_gcn(bias):
            def post(dve, st, g, s):
                rows = NR[:, s, 0:SIZES[g], :]
                st.then(dve.tensor_tensor(rows, rows, TBL[:, gsl(g), :], ALU.add))
                st.then(dve.tensor_tensor(rows, rows, per_node(g), ALU.mult))
                if bias is None:
                    return dve.scalar_tensor_tensor(X[:, gsl(g), :], rows, 0.0, X[:, gsl(g), :],
                                                    ALU.max, ALU.add)
                return dve.tensor_tensor(FE[:, s, 0:SIZES[g], :], rows,
                                         bias_g[:, bias, :].unsqueeze(1).to_broadcast([P, SIZES[g], F]), ALU.add)
            return post

        def per_node(g):
            return dinv[:, gsl(g)].unsqueeze(2).to_broadcast([P, SIZES[g], F])

        def products(g, b=None):
            b = 2 + 2 * (g % 2) if b is None else b
            for t, n in pieces(SIZES[g], 4):
                yield t, n, bank(b + t // 4)[:, 0:n * F].rearrange("p (t f) -> p t f", f=F)

        def plain_rows(act, g):
            for t, n, ps in products(g):
                i = act.copy(TBL[:, gsl(g, t, n), :], ps)
            i.then_inc(table_ready, 1)

        def gcn_rows(dve, g):
            for t, n, ps in products(g):
                i = dve.tensor_tensor(TBL[:, gsl(g, t, n), :], ps,
                                      dinv[:, gsl(g, t, n)].unsqueeze(2).to_broadcast([P, n, F]), ALU.mult)
            i.then_inc(table_ready, 1)

        def edgeconv_rows(bias, theta_bank=2, phi_bank=4):
            def on_v(dve, g):
                for t, n, ps in products(g, phi_bank):
                    i = dve.tensor_tensor(BASE[:, gsl(g, t, n), :], ps,
                                          bias.unsqueeze(1).to_broadcast([P, n, F]), ALU.add)
                i.then_inc(based, 1)

            def on_a(act, g):
                for t, n, ps in products(g, theta_bank):
                    i = act.copy(TBL[:, gsl(g, t, n), :], ps)
                i.then_inc(table_ready, 1)
            return on_v, on_a

        layer(False, idx_sum, post_gcn(None), True, [WT[:, 1, :]], (None, plain_rows), leaders=True,
              scatter=True)

        QI = UNROLL // QUAD
        attr_view = attr_pad.rearrange("(p t) k -> p (t k)", t=T)
        with nc.Block() as block:
            @block.gpsimd
            def _(pool):
                pool.indirect_dma_start(HX[:, 2 * QUAD - 1, :], None, table,
                                        bass.IndirectOffsetOnAxis(first_dst[:].bitcast(u32), 0))\
                    .then_inc(patched, 16)

                def body(it):
                    for j in range(UNROLL):
                        h, a = j // HALF, j % ACCS
                        if j % HALF == 0:
                            hold(pool, staged, it * 2 + h + 1)
                        n = it * (16 * UNROLL // ACCS) + 16 * (j // ACCS)
                        hold(pool, added[a], n)
                        if j % QUAD == 0:
                            hold(pool, totalled, it * QI + j // QUAD + 1)
                        pool.indirect_dma_start(
                            acc_dram[a],
                            bass.IndirectOffsetOnAxis(stage[:, h, j % HALF:j % HALF + 1].bitcast(u32), 0),
                            TOT[:, j // QUAD % 2, a * F:(a + 1) * F], None, compute_op=ALU.add).then_inc(added[a], 16)
                body(0)
                with pool.Fori(1, ITERS) as it:
                    body(it)
                for a in range(ACCS):
                    pool.wait_ge(added[a], 16 * (T // ACCS))

            @block.sync
            def _(sp):
                def fill(c, h, part, used):
                    n = HALF // 2
                    hold(sp, expanded, used)
                    sp.dma_start(FILL[:, h, part * n:(part + 1) * n, :].rearrange("p t f -> p (t f)"),
                                 fill_view[:, ds((c * HALF + part * n) * F, n * F)]).then_inc(fill_in[h], 16)

                def body(it):
                    for h in range(2):
                        c = it * 2 + h
                        fill(c, h, 0, (c - 2) * HALF + HALF // 2)
                        hold(sp, attr_turned, (c - 1) * CQ)
                        sp.dma_start(AT[:, h, :, 0:KA - 1],
                                     attr_view[:, ds(c * HALF * K_ATTR, HALF * K_ATTR)]
                                     .rearrange("p (q k) -> p q k", q=CQ)).then_inc(attr_in[h], 16)
                        hold(sp, spread, (c - 1) * CQ)
                        sp.dma_start(SROW[:, h, :], src_rows[:, ds(c * HALF * P, HALF * P)])\
                            .then_inc(rows_in[h], 16)
                        fill(c, h, 1, (c - 1) * HALF)
                body(0)
                with sp.Fori(1, ITERS) as it:
                    body(it)

            @block.tensor
            def _(pe):
                def turn(it, q):
                    n, q = it * QI + q, q % (2 * QI)
                    h, k = q // CQ % 2, q % CQ
                    if k == 0:
                        pe.wait_ge(attr_in[h], (it + q // QI) * 16 + 16)
                    wait(pe, attr_sb, n)
                    nc.tensor.transpose(bank(0)[0:KA, 0:P], AT[:, h, k, :], ident[:])\
                        .then_inc(attr_turned, 1)

                def spread_src(it, q):
                    n, q = it * QI + q, q % (2 * QI)
                    h, k = q // CQ % 2, q % CQ
                    if k == 0:
                        pe.wait_ge(rows_in[h], (it + q // QI) * 16 + 16)
                    wait(pe, compared, (n - 1) * QUAD)
                    nc.tensor.matmul(bank(6 + q % 2), ones_bf[:], SROW[:, h, k * QUAD * P:(k + 1) * QUAD * P],
                                     start=True, stop=True).then_inc(spread, 1)

                def hide(it, q):
                    n = it * QI + q
                    pe.wait_ge(attr_sb, n + 1)
                    wait(pe, gelu_done, n - 1)
                    for j in range(QUAD):
                        m = nc.tensor.matmul(bank(2 + q % 2)[:, j * P:(j + 1) * P], W1Q[:, j, :],
                                             ATT[:, q % 4, :], start=True, stop=True)
                    m.then_inc(hidden, 1)

                def filters(it, q):
                    n = it * QI + q
                    pe.wait_ge(gelu_done, n + 1)
                    wait(pe, messaged, (n - 1) * QUAD)
                    for j in range(QUAD):
                        o = bank(4 + q % 2)[:, j * F:(j + 1) * F]
                        nc.tensor.matmul(o, GH[:, q % 2, j * P:(j + 1) * P], WF2G[:], start=True, stop=False)
                        m = nc.tensor.matmul(o, ATT[:, q % 4, :], W21Q[:, j, :], start=False, stop=True)
                    m.then_inc(filtered, 1)

                def sum_same(it, q):
                    n = it * QI + q
                    pe.wait_ge(compared, (n + 1) * QUAD)
                    pe.wait_ge(messaged, (n + 1) * QUAD)
                    wait(pe, totalled, n)
                    for j in range(QUAD):
                        m = nc.tensor.matmul(bank(1)[:, j * F:(j + 1) * F], SAME[:, q % 4, j, :],
                                             MSG[:, q % 2, j, :], start=True, stop=True)
                    m.then_inc(summed, 1)

                def body(it, first=False, last=False):
                    for q in range(QI):
                        if not last or q + 2 < QI:
                            turn(it, q + 2)
                            spread_src(it, q + 2)
                        if not last or q + 1 < QI:
                            hide(it, q + 1)
                        filters(it, q)
                        if not first or q > 0:
                            if q > 0:
                                sum_same(it, q - 1)
                            else:
                                sum_same(it - 1, QI - 1)
                turn(0, 0)
                turn(0, 1)
                spread_src(0, 0)
                spread_src(0, 1)
                hide(0, 0)
                body(0, first=True)
                with pe.Fori(1, ITERS - 1) as it:
                    body(it)
                body(ITERS - 1, last=True)
                sum_same(ITERS - 1, QI - 1)

            @block.scalar
            def _(act):
                def copy_attr(it, q):
                    n = it * QI + q
                    act.wait_ge(attr_turned, n + 1)
                    wait(act, filtered, n - 3)
                    act.copy(ATT[:, q % 4, :], bank(0)[0:KA, 0:P]).then_inc(attr_sb, 1)

                def gelu(it, q):
                    n = it * QI + q
                    act.wait_ge(hidden, n + 1)
                    wait(act, filtered, n - 1)
                    act.activation(GH[:, q % 2, :], bank(2 + q % 2), ACT.Gelu, scale=SMU_S)\
                        .then_inc(gelu_done, 1)

                def copy_totals(it, q):
                    n = it * QI + q
                    act.wait_ge(summed, n + 1)
                    for a in range(ACCS):
                        wait(act, added[a], (n - 1) * 16)
                    act.copy(TOT[:, q % 2, :], bank(1)).then_inc(totalled, 1)

                def body(it, first=False, last=False):
                    for q in range(QI):
                        if q % CQ == 0:
                            h = q // CQ
                            for a in range(ACCS):
                                wait(act, added[a], (it * 2 + h - 1) * (16 * HALF // ACCS))
                            act.copy(stage[:, h, :], SCAT[:, ds(it * UNROLL + h * HALF, HALF)])\
                                .then_inc(staged, 1)
                        if not last or q + 2 < QI:
                            copy_attr(it, q + 2)
                        if not last or q + 1 < QI:
                            gelu(it, q + 1)
                        if not first or q > 0:
                            if q > 0:
                                copy_totals(it, q - 1)
                            else:
                                copy_totals(it - 1, QI - 1)
                copy_attr(0, 0)
                copy_attr(0, 1)
                gelu(0, 0)
                body(0, first=True)
                with act.Fori(1, ITERS - 1) as it:
                    body(it)
                body(ITERS - 1, last=True)
                copy_totals(ITERS - 1, QI - 1)

            @block.vector
            def _(dve):
                dve.wait_ge(patched, total.patches + 16)

                def expand(it, q):
                    n = it * QI + q
                    h = q // CQ % 2
                    for j in range(QUAD):
                        t, k, s = n * QUAD + j, q % CQ * QUAD + j, q % 2 * QUAD + j
                        if k == 0:
                            dve.wait_ge(fill_in[h], (it + q // QI) * 32 + 32)
                        wait(dve, messaged, t - 2 * QUAD + 1)
                        wait(dve, expanded, t)
                        dve.scalar_tensor_tensor(HX[:, s, :], HX[:, s - 1 if s else 2 * QUAD - 1, :],
                                                 KEEP[:, ds(t, 1)], FILL[:, h, k, :], ALU.mult, ALU.add)\
                            .then_inc(expanded, 1)
                        if j == 0:
                            dve.wait_ge(spread, n + 1)
                            wait(dve, summed, n - 3)
                        dve.scalar_tensor_tensor(SAME[:, q % 4, j, :],
                                                 bank(6 + q % 2)[:, j * P:(j + 1) * P], SRCF[:, ds(t, 1)],
                                                 lower[:], ALU.is_equal, ALU.mult).then_inc(compared, 1)

                def message(it, q):
                    n = it * QI + q
                    dve.wait_ge(filtered, n + 1)
                    wait(dve, summed, n - 1)
                    dve.wait_ge(expanded, (n + 1) * QUAD)
                    for j in range(QUAD):
                        dve.scalar_tensor_tensor(MSG[:, q % 2, j, :],
                                                 bank(4 + q % 2)[:, j * F:(j + 1) * F],
                                                 WEIGHT[:, ds(n * QUAD + j, 1)], HX[:, q % 2 * QUAD + j, :],
                                                 ALU.mult, ALU.mult).then_inc(messaged, 1)

                def body(it, last=False):
                    for q in range(QI):
                        if not last or q + 1 < QI:
                            expand(it, q + 1)
                        message(it, q)
                expand(0, 0)
                body(0)
                with dve.Fori(1, ITERS - 1) as it:
                    body(it)
                body(ITERS - 1, last=True)
        clear()
        total.patches += 16

        def post_edgeconv(onto_x):
            def post(dve, st, g, s):
                rows = NR[:, s, 0:SIZES[g], :]
                st.then(dve.tensor_tensor(rows, rows, BASE[:, gsl(g), :], ALU.add))
                if onto_x:
                    return dve.scalar_tensor_tensor(X[:, gsl(g), :], rows, 0.0, X[:, gsl(g), :],
                                                    ALU.max, ALU.add)
                return dve.tensor_single_scalar(FE[:, s, 0:SIZES[g], :], rows, 0.0, ALU.max)
            return post

        WE_flat = WE[:, :, :].rearrange("p l f -> p (l f)")
        bias_flat = bias_e[:, :, :].rearrange("p l f -> p (l f)")
        gelu_part = G[:, :, :]
        linear_part = TOT[:, :, :].rearrange("p a (b f) -> p (a b) f", f=F)
        on_v, on_a = edgeconv_rows(bias_e[:, 0, :], 6, 0)
        with nc.Block() as block:
            @block.sync
            def _(sp):
                def table_rows(g):
                    sp.wait_ge(table_ready, g + 1)
                    sp.dma_start(group_rows(table, g), TBL[:, gsl(g), :]).then_inc(table_out, 16)
                for g in range(NG):
                    s = g % 2
                    wait(sp, agg_turned, g - 1)
                    for k in range(ACCS):
                        sp.dma_start(ACC[:, s, k, 0:SIZES[g], :], group_rows(acc_dram[k], g))\
                            .then_inc(acc_in[s], 16)
                    if g >= 4:
                        table_rows(g - 4)
                for g in range(NG - 4, NG):
                    table_rows(g)
                sp.wait_ge(table_out, 16 * NG)

            @block.vector
            def _(dve):
                st = Steps(dve, order_v)

                def sums(g):
                    acc = [ACC[:, g % 2, k, 0:SIZES[g], :] for k in range(ACCS)]
                    dve.wait_ge(acc_in[g % 2], 16 * ACCS * (g // 2 + 1))
                    st.did(dve.tensor_tensor(acc[0], acc[0], acc[1], ALU.add))
                    st.did(dve.tensor_tensor(acc[2], acc[2], acc[3], ALU.add))
                    st.join()
                    dve.tensor_tensor(acc[0], acc[0], acc[2], ALU.add).then_inc(rows_used, 1)

                sums(0)
                for g in range(NG + 2):
                    if g + 1 < NG:
                        sums(g + 1)
                    if 1 <= g <= NG:
                        a = g - 1
                        dve.wait_ge(agg_projected, a + 1)
                        for t, n, ps in products(a, 4):
                            k = gsl(a, t, n)
                            i = dve.tensor_tensor(X[:, k, :], X[:, k, :], ps, ALU.add)
                            i.then_inc(evicted, 1) if t + n == SIZES[a] else st.did(i)
                        st.join()
                        dve.wait_ge(evicted, a + 1)
                        st.then(dve.tensor_tensor(X[:, gsl(a), :], X[:, gsl(a), :], bias_o2[:, :].unsqueeze(1)
                                                  .to_broadcast([P, SIZES[a], F]), ALU.add))
                        node_stats(dve, st, a)
                    if g >= 2:
                        dve.wait_ge(projected, g - 1)
                        on_v(dve, g - 2)
                    if 1 <= g <= NG:
                        node_scale(dve, st, g - 1)

            @block.tensor
            def _(pe):
                for g in range(NG + 2):
                    s = g % 2
                    if g < NG:
                        pe.wait_ge(rows_used, g + 1)
                        wait(pe, based, g - 2)
                        turn_features(pe, g, 0, lambda t: ACC[:, s, 0, t, :]).then_inc(agg_turned, 1)
                    if g >= 2:
                        pe.wait_ge(feat_ready, g - 1)
                        wait(pe, table_ready, g - 2)
                        turn_features(pe, g - 2, 6).then_inc(turned, 1)
                    if g < NG:
                        pe.wait_ge(agg_sb, g + 1)
                        wait(pe, gelu_done, g)
                        for t, n in pieces(SIZES[g], 4):
                            m = nc.tensor.matmul(bank(2 + t // 4)[:, 0:n * P], WO1[:],
                                                 NR[:, s, t:t + n, :].rearrange("p t f -> p (t f)"),
                                                 start=True, stop=True)
                        m.then_inc(hidden, 1)
                    if g >= 2:
                        b = g - 2
                        pe.wait_ge(turned_sb, b + 1)
                        wait(pe, based, b)
                        for k, first in enumerate((6, 0)):
                            for t in range(SIZES[b]):
                                m = nc.tensor.matmul(bank(first + t // 4)[:, t % 4 * F:(t % 4 + 1) * F],
                                                     FT[:, b % 2, t * P:(t + 1) * P],
                                                     WE[:, 0, k * F:(k + 1) * F], start=True, stop=True)
                        m.then_inc(projected, 1)
                    if g < NG:
                        pe.wait_ge(gelu_done, g + 1)
                        wait(pe, evicted, g)
                        for t in range(SIZES[g]):
                            o = bank(4 + t // 4)[:, t % 4 * F:(t % 4 + 1) * F]
                            nc.tensor.matmul(o, gelu_part[:, t, :], WO2G[:], start=True, stop=False)
                            m = nc.tensor.matmul(o, linear_part[:, t, :], WO2L[:], start=False, stop=True)
                        m.then_inc(agg_projected, 1)

            @block.scalar
            def _(act):
                for g in range(NG + 2):
                    s = g % 2
                    if g < NG:
                        act.wait_ge(agg_turned, g + 1)
                        for t, n in pieces(SIZES[g], 4):
                            i = act.copy(NR[:, s, t:t + n, :].rearrange("p t f -> p (t f)"),
                                         bank(t // 4)[:, 0:n * P])
                        i.then_inc(agg_sb, 1)
                    if g >= 2:
                        copy_turned(act, g - 2, 6)
                    if g < NG:
                        act.wait_ge(hidden, g + 1)
                        for t, n in pieces(SIZES[g], 4):
                            ps = bank(2 + t // 4)[:, 0:n * P].rearrange("p (t f) -> p t f", f=P)
                            act.activation(gelu_part[:, t:t + n, :], ps, ACT.Gelu, bias=cols[:, 5:6], scale=SMU_S)
                            i = act.activation(linear_part[:, t:t + n, :], ps, ACT.Identity, bias=cols[:, 4:5])
                        i.then_inc(gelu_done, 1)
                    if g >= 2:
                        act.wait_ge(projected, g - 1)
                        on_a(act, g - 2)
                    if 1 <= g <= NG:
                        node_norm(act, g - 1)
        clear()
        with nc.Fori(0, LAYERS - 1) as l:
            layer(True, idx_max, post_edgeconv(False), False,
                  [WE_flat[:, ds((2 * l + 2 + k) * F, F)] for k in range(2)],
                  edgeconv_rows(bias_flat[:, ds((l + 1) * F, F)]), times=l, runs=LAYERS - 1)
        layer(True, idx_max, post_edgeconv(True), True, [W12[:, 0, :]], (gcn_rows, None))

        layer(False, idx_sum, post_gcn(0), False, [W12[:, 1, :]], (gcn_rows, None))
        last = passing(False, 0, total.patches)
        base = list(total.rows)
        with nc.Block() as block:
            @block.gpsimd
            def _(pool):
                last["pool"](pool)
                for g in range(NG):
                    s = g % 2
                    wait(pool, rows_used, g - 1)
                    for t in range(SIZES[g]):
                        k = STARTS[g] + t
                        pool.indirect_dma_start(NR[:, s, t, :], None, run_rows,
                                                table_row(run_rows, idx_sum[:, k:k + 1]))\
                            .then_inc(rows_landed[s], 16)

            @block.vector
            def _(dve):
                st = Steps(dve, order_v)
                last["dve"](dve, st)
                for g in range(NG):
                    s = g % 2
                    rows = NR[:, s, 0:SIZES[g], :]
                    dve.wait_ge(rows_landed[s], base[s] + 16 * sum(SIZES[s:g + 1:2]))
                    st.then(dve.tensor_tensor(rows, rows, TBL[:, gsl(g), :], ALU.add))
                    st.then(dve.tensor_tensor(rows, rows, per_node(g), ALU.mult))
                    st.then(dve.tensor_tensor(rows, rows, bias_g[:, 1, :].unsqueeze(1)
                                              .to_broadcast([P, SIZES[g], F]), ALU.add))
                    dve.tensor_tensor(X[:, gsl(g), :], X[:, gsl(g), :], rows, ALU.add).then_inc(rows_used, 1)

            @block.scalar
            def _(act):
                last["act"](act)

            @block.tensor
            def _(pe):
                last["pe"](pe)

            @block.sync
            def _(sp):
                last["sp"](sp)
                for g in range(NG):
                    sp.wait_ge(rows_used, g + 1)
                    a, b = gsl(g).start, min(gsl(g).stop, N // P)
                    sp.dma_start(out[a * P:b * P, :].rearrange("(t p) f -> p t f", p=P), X[:, a:b, :])\
                        .then_inc(table_out, 16)
                sp.dma_start(out[N // P * P:N, :], X[0:N % P, NT - 1, :]).then_inc(table_out, 16)
                sp.wait_ge(table_out, 16 * (NG + 1))


_INS = ["x", "src", "dst", "edge_attr_20", "edge_weight", "L0_gnn_W", "L0_gnn_b", "L0_gnn_gamma",
        "L0_gnn_beta", "L1_gnn_W_in2f", "L1_gnn_W_f1", "L1_gnn_b_f1", "L1_gnn_W_f2", "L1_gnn_b_f2",
        "L1_gnn_W_o1", "L1_gnn_b_o1", "L1_gnn_W_o2", "L1_gnn_b_o2", "L2_gnn_theta_w", "L2_gnn_theta_b",
        "L2_gnn_phi_w", "L2_gnn_phi_b", "L3_gnn_W1", "L3_gnn_b1", "L3_gnn_W2", "L3_gnn_b2"]


def kernel(**inputs):
    import numpy as np
    import concourse.bacc as bacc
    from concourse.bass_utils import run_bass_kernel_spmd

    nc = bacc.Bacc("TRN2", target_bir_lowering=False, num_devices=1)
    arrays, args = {}, []
    for name in _INS:
        a = np.ascontiguousarray(inputs[name])
        arrays[f"in_{name}"] = a
        args.append(nc.dram_tensor(f"in_{name}", a.shape, mybir.dt.from_np(a.dtype), kind="ExternalInput").ap())
    out = nc.dram_tensor("out", (N, F), mybir.dt.float32, kind="ExternalOutput").ap()
    gnn_kernel(nc, *args, out)
    return run_bass_kernel_spmd(nc, [arrays], core_ids=[0]).results[0]["out"]
```
